# Optimizing a Trainium2 kernel written in Bass

```python
import numpy as np
import jax
import jax.numpy as jnp

def _softmax(x, axis=-1):
    return jax.nn.softmax(x, axis=axis)

def _gelu(x):
    return jax.nn.gelu(x, approximate=True)

def _silu(x):
    return jax.nn.silu(x)

def _sigmoid(x):
    return jax.nn.sigmoid(x)

def _layernorm(x, axis=-1, eps=1e-05):
    m = jnp.mean(x, axis=axis, keepdims=True)
    v = jnp.var(x, axis=axis, keepdims=True)
    return (x - m) / jnp.sqrt(v + eps)

def _scatter_add(tgt, idx, src, axis=0):
    return tgt.at[idx].add(src)

def _segment_sum(src, seg, n):
    return jax.ops.segment_sum(src, seg, n)
kernel_name = 'mk_seq_postln_d1_jaxref_r8_aeb6fc'

def setup_inputs(seed: int=0):
    np.random.seed(seed)
    _w = jnp.asarray

    def _L0_attn_setup():
        import jax, jax.numpy as jnp
        import numpy as np
        D_MODEL, N_HEADS, N_KV, HEAD_DIM, D_LAT = (128, 8, 2, 128, 32)
        N_REP = N_HEADS // N_KV
        B, T = (2, 256)
        key = jax.random.key(seed)
        ks = jax.random.split(key, 8)
        s = lambda fan_in: 1.0 / np.sqrt(fan_in)
        return {'x': jax.random.normal(ks[0], (B, T, D_MODEL), jnp.float32), 'wq': jax.random.normal(ks[1], (D_MODEL, N_HEADS * HEAD_DIM), jnp.float32) * s(D_MODEL), 'wk_down': jax.random.normal(ks[2], (D_MODEL, N_KV * D_LAT), jnp.float32) * s(D_MODEL), 'wv_down': jax.random.normal(ks[3], (D_MODEL, N_KV * D_LAT), jnp.float32) * s(D_MODEL), 'wk_up': jax.random.normal(ks[4], (D_LAT, HEAD_DIM), jnp.float32) * s(D_LAT), 'wv_up': jax.random.normal(ks[5], (D_LAT, HEAD_DIM), jnp.float32) * s(D_LAT), 'wo': jax.random.normal(ks[6], (N_HEADS * HEAD_DIM, D_MODEL), jnp.float32) * s(N_HEADS * HEAD_DIM)}
    _L0_attn_in = _L0_attn_setup()

    def _L0_ffn_setup():
        import jax, jax.numpy as jnp
        import numpy as np
        TOP_K = 2
        EPS = 1e-05

        def layer_norm(x, g, b):
            mu = jnp.mean(x, axis=-1, keepdims=True)
            var = jnp.mean(jnp.square(x - mu), axis=-1, keepdims=True)
            return (x - mu) * jax.lax.rsqrt(var + EPS) * g + b
        key = jax.random.key(seed)
        ks = jax.random.split(key, 12)
        B, S, D, F, E = (2, 256, 128, 512, 8)
        std = 0.02
        return {'x': jax.random.normal(ks[0], (B, S, D), jnp.float32), 'g1': jnp.ones((D,), jnp.float32), 'be1': jnp.zeros((D,), jnp.float32), 'mix_w': jax.random.normal(ks[1], (D, D), jnp.float32) * std, 'mix_b': jnp.zeros((D,), jnp.float32), 'g2': jnp.ones((D,), jnp.float32), 'be2': jnp.zeros((D,), jnp.float32), 'router_w': jax.random.normal(ks[2], (D, E), jnp.float32) * std, 'w1': jax.random.normal(ks[3], (E, D, F), jnp.float32) * std, 'b1': jnp.zeros((E, F), jnp.float32), 'w2': jax.random.normal(ks[4], (E, F, D), jnp.float32) * std, 'b2': jnp.zeros((E, D), jnp.float32)}
    _L0_ffn_in = _L0_ffn_setup()
    _d = {'L0_attn_x': _L0_attn_in['x'], 'L0_attn_wq': _L0_attn_in['wq'], 'L0_attn_wk_down': _L0_attn_in['wk_down'], 'L0_attn_wv_down': _L0_attn_in['wv_down'], 'L0_attn_wk_up': _L0_attn_in['wk_up'], 'L0_attn_wv_up': _L0_attn_in['wv_up'], 'L0_attn_wo': _L0_attn_in['wo'], 'L0_ffn_g1': _L0_ffn_in['g1'], 'L0_ffn_be1': _L0_ffn_in['be1'], 'L0_ffn_mix_w': _L0_ffn_in['mix_w'], 'L0_ffn_mix_b': _L0_ffn_in['mix_b'], 'L0_ffn_g2': _L0_ffn_in['g2'], 'L0_ffn_be2': _L0_ffn_in['be2'], 'L0_ffn_router_w': _L0_ffn_in['router_w'], 'L0_ffn_w1': _L0_ffn_in['w1'], 'L0_ffn_b1': _L0_ffn_in['b1'], 'L0_ffn_w2': _L0_ffn_in['w2'], 'L0_ffn_b2': _L0_ffn_in['b2']}
    _x0 = _d['L0_attn_x']
    _d['L0_attn_x'] = jax.random.normal(jax.random.fold_in(jax.random.key(seed), 1), (32, 256, 128), dtype=_x0.dtype)
    del _x0
    return _d

def reference(L0_attn_x, L0_attn_wq, L0_attn_wk_down, L0_attn_wv_down, L0_attn_wk_up, L0_attn_wv_up, L0_attn_wo, L0_ffn_g1, L0_ffn_be1, L0_ffn_mix_w, L0_ffn_mix_b, L0_ffn_g2, L0_ffn_be2, L0_ffn_router_w, L0_ffn_w1, L0_ffn_b1, L0_ffn_w2, L0_ffn_b2):

    def _L0_attn_ref(x, wq, wk_down, wv_down, wk_up, wv_up, wo):
        import jax, jax.numpy as jnp
        import numpy as np
        D_MODEL, N_HEADS, N_KV, HEAD_DIM, D_LAT = (128, 8, 2, 128, 32)
        N_REP = N_HEADS // N_KV
        B, T = (2, 256)
        Bq, Tq, _ = x.shape
        scale = HEAD_DIM ** (-0.5)
        q = (x @ wq).reshape(Bq, Tq, N_KV, N_REP, HEAD_DIM)
        k_lat = (x @ wk_down).reshape(Bq, Tq, N_KV, D_LAT)
        v_lat = (x @ wv_down).reshape(Bq, Tq, N_KV, D_LAT)
        k = jnp.einsum('bkhl,ld->bkhd', k_lat, wk_up)
        v = jnp.einsum('bkhl,ld->bkhd', v_lat, wv_up)
        scores = jnp.einsum('bqhrd,bkhd->bhrqk', q, k) * scale
        causal = jnp.tril(jnp.ones((Tq, Tq), dtype=bool))
        scores = jnp.where(causal, scores, jnp.finfo(scores.dtype).min)
        probs = jax.nn.softmax(scores, axis=-1)
        y = jnp.einsum('bhrqk,bkhd->bqhrd', probs, v)
        y = y.reshape(Bq, Tq, N_HEADS * HEAD_DIM)
        return y @ wo

    def _L0_ffn_ref(x, g1, be1, mix_w, mix_b, g2, be2, router_w, w1, b1, w2, b2):
        import jax, jax.numpy as jnp
        import numpy as np
        TOP_K = 2
        EPS = 1e-05

        def layer_norm(x, g, b):
            mu = jnp.mean(x, axis=-1, keepdims=True)
            var = jnp.mean(jnp.square(x - mu), axis=-1, keepdims=True)
            return (x - mu) * jax.lax.rsqrt(var + EPS) * g + b
        res = x
        n = layer_norm(x, g1, be1)
        x = res + n + (n @ mix_w + mix_b)
        res = x
        n = layer_norm(x, g2, be2)
        B, S, D = n.shape
        E = w1.shape[0]
        flat = n.reshape(-1, D)
        probs = jax.nn.softmax(flat @ router_w, axis=-1)
        topw, topi = jax.lax.top_k(probs, TOP_K)
        combine = jnp.sum(jax.nn.one_hot(topi, E, dtype=flat.dtype) * topw[..., None], axis=1)
        h = jax.nn.silu(jnp.einsum('td,edf->tef', flat, w1) + b1)
        y = jnp.einsum('tef,efd->ted', h, w2) + b2
        out = jnp.einsum('te,ted->td', combine, y)
        return res + out.reshape(B, S, D)
    x = L0_attn_x
    x = _layernorm(x + _L0_attn_ref(x, L0_attn_wq, L0_attn_wk_down, L0_attn_wv_down, L0_attn_wk_up, L0_attn_wv_up, L0_attn_wo), axis=-1)
    x = _layernorm(x + _L0_ffn_ref(x, L0_ffn_g1, L0_ffn_be1, L0_ffn_mix_w, L0_ffn_mix_b, L0_ffn_g2, L0_ffn_be2, L0_ffn_router_w, L0_ffn_w1, L0_ffn_b1, L0_ffn_w2, L0_ffn_b2), axis=-1)
    return x

_drawn_inputs = setup_inputs


def setup_inputs(seed=0):
    import zlib

    import numpy as np

    out = dict(_drawn_inputs(seed))
    spreads = {'L0_ffn_g1': (1.0, 0.2),
     'L0_ffn_be1': (0.0, 0.1),
     'L0_ffn_mix_b': (0.0, 0.1),
     'L0_ffn_g2': (1.0, 0.6),
     'L0_ffn_be2': (0.0, 0.8),
     'L0_ffn_b1': (0.0, 0.8),
     'L0_ffn_b2': (0.0, 0.8)}
    factors = {'L0_ffn_router_w': 7.694, 'L0_ffn_w1': 8.0, 'L0_ffn_w2': 8.0}
    for name, (base, spread) in spreads.items():
        noise = np.random.default_rng([zlib.crc32(name.encode()), seed]).standard_normal(out[name].shape)
        drawn = base * np.exp(spread * noise) if base else spread * noise
        out[name] = jnp.asarray(drawn.astype(out[name].dtype))
    for name, factor in factors.items():
        out[name] = (out[name] * factor).astype(out[name].dtype)
    return out
```

```python
from contextlib import ExitStack

import concourse.bass as bass
from concourse import mybir

F32 = mybir.dt.float32
F32R = mybir.dt.float32r
BF16 = mybir.dt.bfloat16
ALU = mybir.AluOpType
ACT = mybir.ActivationFunctionType
AX = mybir.AxisListType

P = 128
EPS = 1e-5
MASKED = -1e30
HEADS = 8
GROUPS = 2
REP = HEADS // GROUPS
LAT = 32
EXPERTS = 8
ACT_HEADS = (0, 2, 3, 5, 6)


class Batch:

    def __init__(self, pair, off, count):
        self.pair, self.off, self.count = pair, off, count
        self.parity = off % 2

    def shift(self, d):
        return Batch(self.pair, self.off + d, self.count)

    def exists(self):
        return not isinstance(self.pair, int) or 0 <= 2 * self.pair + self.off < self.count

    def n(self, per, k=0):
        if per == 0:
            return k
        return self.pair * (2 * per) + (self.off * per + k)

    def uses(self, per=16):
        return self.pair * per + (self.off // 2 + 1) * per


def wait(eng, sem, value):
    if not isinstance(value, int) or value > 0:
        eng.wait_ge(sem, value)


def wait_apart(eng, sem, value, apart):
    if not isinstance(value, int) or value > 0:
        eng.wait_ge(sem, value)
        eng.sem_inc(apart)


def pairs_of(eng, batches, step, before=1, after=2):
    for i in range(-before, 4):
        step(Batch(0, i, batches))
    with eng.Fori(2, batches // 2 - 1) as j:
        step(Batch(j, 0, batches))
        step(Batch(j, 1, batches))
    for i in range(batches - 2, batches + after):
        step(Batch(0, i, batches))


def build(nc, x, wq, wk_down, wv_down, wk_up, wv_up, wo, g1, be1, mix_w, mix_b, g2, be2, router_w, w1, b1, w2, b2, out):
    NB, T, D = x.shape
    F = w1.shape[2]
    FT = F // P
    QT = T // P
    assert D == P and QT == 2 and NB % 2 == 0 and FT == 4
    TILES = NB * QT
    SCALE = float(P) ** -0.5
    HB = HEADS

    x_t = x.rearrange("b (t p) d -> b p t d", p=P)
    out_t = out.rearrange("b (t p) d -> b p t d", p=P)
    x2_d = nc.dram_tensor("x2_scratch", [NB, P, QT, D], F32).ap()
    z2t_d = nc.dram_tensor("z2t_scratch", [NB, P, T], F32).ap()

    with ExitStack() as ctx:
        def sb(name, shape, dt=F32):
            return ctx.enter_context(nc.sbuf_tensor(name, shape, dt))

        def sem(name):
            return ctx.enter_context(nc.semaphore(name))

        bank = [ctx.enter_context(nc.psum_tensor(f"bank{i}", [P, 512], F32)) for i in range(8)]
        SC, PT, YL, PA, PC = bank[0:2], bank[2:4], bank[4:6], bank[6], bank[7]

        ident = sb("ident", [P, P])
        ident_bf = sb("ident_bf", [P, P], BF16)
        mask_bf = sb("mask_bf", [P, P], BF16)
        half_neg = sb("half_neg", [P, QT])
        iota_down = sb("iota_down", [P, EXPERTS])
        wq_sb = sb("wq_sb", [P, HEADS, P])
        wo_sb = sb("wo_sb", [P, HEADS, P])
        wkv_sb = sb("wkv_sb", [P, 2, GROUPS, LAT])
        up_sb = sb("up_sb", [LAT, 2, P])
        vec_sb = sb("vec_sb", [36, P])
        upT = sb("upT", [P, 2, LAT])
        wqT = sb("wqT", [P, HEADS, P])
        absq = sb("absq", [P, HEADS, LAT])
        wq_hi = sb("wq_hi", [P, HEADS, 3, LAT], F32R)
        wq_lo = sb("wq_lo", [P, HEADS, 3, LAT], F32R)
        wkv_hi = sb("wkv_hi", [P, GROUPS, 4, LAT], F32R)
        wkv_lo = sb("wkv_lo", [P, GROUPS, 4, LAT], F32R)
        wvo = sb("wvo", [P, GROUPS, P])
        vecT = sb("vecT", [P, 36])
        mix_sb = sb("mix_sb", [P, P])
        mixb_bc = sb("mixb_bc", [P, P])
        m1 = sb("m1", [P, P])
        c1 = sb("c1", [P, P])
        rw_sb = sb("rw_sb", [P, EXPERTS])
        rg = sb("rg", [P, EXPERTS])
        rb = sb("rb", [P, EXPERTS])
        bcol = sb("bcol", [P, 2, P])
        w1_sb = sb("w1_sb", [P, EXPERTS, F])
        w2_sb = sb("w2_sb", [P, EXPERTS, FT, D])
        b2_bc = sb("b2_bc", [P, EXPERTS, D])
        b1T = sb("b1T", [P, EXPERTS * FT])

        xq = sb("xq", [P, 2, QT, D])
        xr = sb("xr", [P, 2, QT, D])
        xT_hi = sb("xT_hi", [P, T], F32R)
        xT_lo = sb("xT_lo", [P, T], F32R)
        qs = sb("qs", [P, 2, HEADS, T], F32R)
        ks = sb("ks", [P, 2, GROUPS, T], F32R)
        vT = sb("vT", [P, GROUPS, T])
        v_sb = sb("v_sb", [P, 2, QT, GROUPS, LAT])
        negm = sb("negm", [P, 2, QT, HEADS])
        sums = sb("sums", [P, 2, QT, HEADS])
        recips = sb("recips", [P, 2, QT, HEADS])
        recb = sb("recb", [P, QT, HEADS, LAT])
        probs = sb("probs", [P, 4, 3 * P])
        probsT = sb("probsT", [P, 4, 3 * P])
        rs_sb = sb("rs_sb", [P, GROUPS, T])
        ylT = sb("ylT", [P, GROUPS, T])

        a_sb = sb("a_sb", [P, QT, D])
        st1 = sb("st1", [P, QT, 6])
        mv1 = sb("mv1", [P, QT, 2])
        ve1 = sb("ve1", [P, QT])
        r1 = sb("r1", [P, QT])
        u1 = sb("u1", [P, 3, QT])
        rr1 = sb("rr1", [P, QT])
        x1 = sb("x1", [P, QT, D])
        x1c = sb("x1c", [P, QT, D])
        x1T = sb("x1T", [P, T])
        x2 = sb("x2", [P, 2, QT, D])
        x12 = sb("x12", [P, 2, QT, D])
        st2 = sb("st2", [P, QT, 6])
        mv2 = sb("mv2", [P, QT, 2])
        ve2 = sb("ve2", [P, QT])
        r2 = sb("r2", [P, QT])
        z2 = sb("z2", [P, QT, D])
        z2T = sb("z2T", [P, 2, T])
        logits = sb("logits", [P, TILES, EXPERTS])

        rt = [sb(f"rt{i}", [P, TILES, EXPERTS]) for i in range(4)]
        rs1 = [sb(f"rs1_{i}", [P, TILES]) for i in range(4)]
        comb = sb("comb", [P, TILES, EXPERTS])

        zin = sb("zin", [P, 2, T])
        xin = sb("xin", [P, 2, QT, D])
        hT = sb("hT", [P, 2, FT, T])
        acc = sb("acc", [P, QT, D])
        st3 = sb("st3", [P, QT, 6])
        mv3 = sb("mv3", [P, QT, 2])
        ve3 = sb("ve3", [P, QT])
        r3 = sb("r3", [P, QT])
        o_sb = sb("o_sb", [P, 2, QT, D])

        names = ("w_in0 w_in1 w_in2 w_in3 w_in4 const_ready set_pe set_act set_dve xq_in0 xq_in1 xr_in0 xr_in1 "
                 "s1_pe s1_act s1_dve sc_done max_done exp_done pt_done pt_act pt_dve pv_done "
                 "s3_pe s3_act s3_dve s3_pool x2_out0 x2_out1 z_out0 z_out1 route_dve route_act "
                 "apart_pool apart_pe apart_dve zin0 zin1 xin0 xin1 h_done silu_done y_done acc_done fin_dve fin_pool o_out0 o_out1").split()
        S = {n: sem(n) for n in names}
        xq_in = [S["xq_in0"], S["xq_in1"]]
        xr_in = [S["xr_in0"], S["xr_in1"]]
        x2_out = [S["x2_out0"], S["x2_out1"]]
        z_out = [S["z_out0"], S["z_out1"]]
        zin_s = [S["zin0"], S["zin1"]]
        xin_s = [S["xin0"], S["xin1"]]
        o_out = [S["o_out0"], S["o_out1"]]
        w_in = [S[f"w_in{i}"] for i in range(5)]
        const_ready, set_pe, set_act, set_dve = (S[n] for n in "const_ready set_pe set_act set_dve".split())
        s1_pe, s1_act, s1_dve = S["s1_pe"], S["s1_act"], S["s1_dve"]
        sc_done, max_done, exp_done, pt_done, pv_done = (S[n] for n in "sc_done max_done exp_done pt_done pv_done".split())
        pt_act, pt_dve = S["pt_act"], S["pt_dve"]
        s3_pe, s3_act, s3_dve, s3_pool = (S[n] for n in "s3_pe s3_act s3_dve s3_pool".split())
        route_dve, route_act = S["route_dve"], S["route_act"]
        h_done, silu_done, y_done, acc_done = (S[n] for n in "h_done silu_done y_done acc_done".split())
        fin_dve, fin_pool = S["fin_dve"], S["fin_pool"]

        NA = len(ACT_HEADS)
        ND = HEADS - NA
        S1 = 7
        PE3, ACT3, DVE3, POOL3 = 6, 3, 14, 15
        SET_DVE = 15

        def copied(eng, b, h):
            if h in ACT_HEADS:
                wait(eng, pt_act, b.n(NA, sum(k <= h for k in ACT_HEADS)))
            else:
                wait(eng, pt_dve, b.n(ND, sum(k <= h and k not in ACT_HEADS for k in range(HEADS))))

        def lag(b, h, d):
            return (b, h - d) if h >= d else (b.shift(-1), h - d + HEADS)

        block = ctx.enter_context(nc.Block())

        @block.sync
        def _(sp):
            sp.dma_start(wq_sb[:], wq.rearrange("d (h k) -> d h k", h=HEADS)).then_inc(w_in[0], 16)
            sp.dma_start(up_sb[:, 0, :], wk_up).then_inc(w_in[0], 16)
            sp.dma_start(up_sb[:, 1, :], wv_up).then_inc(w_in[0], 16)
            sp.dma_start(wkv_sb[:, 0], wk_down.rearrange("d (g l) -> d g l", g=GROUPS)).then_inc(w_in[0], 16)
            sp.dma_start(wkv_sb[:, 1], wv_down.rearrange("d (g l) -> d g l", g=GROUPS)).then_inc(w_in[0], 16)
            sp.dma_start(wo_sb[:], wo.rearrange("(h k) d -> k h d", h=HEADS)).then_inc(w_in[1], 16)
            sp.dma_start(vec_sb[0:32, :], b1.rearrange("e (f p) -> (e f) p", p=P)).then_inc(w_in[2], 16)
            for n, v in enumerate((g1, be1, g2, be2)):
                sp.dma_start(vec_sb[32 + n:33 + n, :], v.rearrange("(a d) -> a d", a=1)).then_inc(w_in[2], 16)
            sp.dma_start(mix_sb[:], mix_w).then_inc(w_in[2], 16)
            sp.dma_start(mixb_bc[:], mix_b.partition_broadcast(P)).then_inc(w_in[2], 16)
            sp.dma_start(rw_sb[:], router_w).then_inc(w_in[2], 16)
            sp.dma_start(w1_sb[:], w1.rearrange("e d f -> d e f")).then_inc(w_in[3], 16)
            sp.dma_start(w2_sb[:], w2.rearrange("e (f p) d -> p e f d", p=P)).then_inc(w_in[4], 16)
            sp.dma_start(b2_bc[:], b2.partition_broadcast(P)).then_inc(w_in[4], 16)

            def step(i):
                c, p = i.shift(1), i.shift(1).parity
                if c.exists():
                    wait(sp, s1_pe, c.n(S1, 1 - 2 * S1))
                    sp.dma_start(xq[:, p], x_t[dyn(c)]).then_inc(xq_in[p], 16)
                c, p = i, i.parity
                if c.exists():
                    wait(sp, s3_dve, c.n(DVE3, 3 - 2 * DVE3))
                    sp.dma_start(xr[:, p], x_t[dyn(c)]).then_inc(xr_in[p], 16)
                c, p = i.shift(-2), i.parity
                if c.exists():
                    wait(sp, s3_pool, c.n(POOL3, 15))
                    sp.dma_start(x2_d[dyn(c)], x12[:, p]).then_inc(x2_out[p], 16)
                    wait(sp, s3_act, c.n(ACT3, 3))
                    sp.dma_start(z2t_d[dyn(c)], z2T[:, p]).then_inc(z_out[p], 16)

            def dyn(c):
                return c.n(1)

            pairs_of(sp, NB, step)
            for p in range(2):
                sp.wait_ge(x2_out[p], 16 * NB // 2)
                sp.wait_ge(z_out[p], 16 * NB // 2)

            def step(i):
                c, p = i.shift(1), i.shift(1).parity
                if c.exists():
                    wait(sp, y_done, c.n(EXPERTS, -EXPERTS))
                    sp.dma_start(zin[:, p], z2t_d[dyn(c)]).then_inc(zin_s[p], 16)
                    wait(sp, fin_dve, c.n(6, -6))
                    sp.dma_start(xin[:, p], x2_d[dyn(c)]).then_inc(xin_s[p], 16)
                c, p = i.shift(-1), i.shift(-1).parity
                if c.exists():
                    wait(sp, fin_dve, c.n(6, 6))
                    sp.dma_start(out_t[dyn(c)], o_sb[:, p]).then_inc(o_out[p], 16)

            pairs_of(sp, NB, step, after=1)
            for p in range(2):
                sp.wait_ge(o_out[p], 16 * NB // 2)

        @block.gpsimd
        def _(pool):
            pool.memset(ident[:], 0.0).then_inc(const_ready, 1)
            pool.memset(mask_bf[:], 0.0).then_inc(const_ready, 1)
            pool.memset(half_neg[:], -0.5).then_inc(const_ready, 1)
            pool.iota(iota_down[:], pattern=[[-1, EXPERTS]], base=EXPERTS, channel_multiplier=0,
                      allow_small_or_imprecise_dtypes=True).then_inc(const_ready, 1)
            pool.wait_ge(const_ready, 4)
            pool.affine_select(out=ident[:], in_=ident[:], compare_op=ALU.not_equal, fill=1.0,
                               base=0, pattern=[[-1, P]], channel_multiplier=1).then_inc(const_ready, 1)
            pool.affine_select(out=mask_bf[:], in_=mask_bf[:], compare_op=ALU.is_ge, fill=MASKED,
                               base=0, pattern=[[-1, P]], channel_multiplier=1).then_inc(const_ready, 1)
            pool.wait_ge(const_ready, 6)
            pool.tensor_copy(ident_bf[:], ident[:]).then_inc(const_ready, 1)

            def wait(eng, sem, value):
                wait_apart(eng, sem, value, S["apart_pool"])

            def step(i):
                c = i.shift(-1)
                if c.exists():
                    def then(ins, k):
                        ins.then_inc(s3_pool, 1)

                    wait(pool, s3_dve, c.n(DVE3, 1))
                    wait(pool, s3_pe, c.n(PE3, 1 - PE3))
                    then(pool.tensor_copy(recb[:], recips[:, c.parity].unsqueeze(3).broadcast_to([P, QT, HEADS, LAT])), 0)
                    wait(pool, s3_dve, c.n(DVE3, 7))
                    then(pool.tensor_scalar(ve1[:], mv1[:, :, 1], EPS, None, ALU.add, ALU.bypass), 1)
                    wait(pool, s3_pool, c.n(POOL3, 2))
                    then(pool.tensor_tensor(r1[:], ve1[:], half_neg[:], ALU.pow), 2)
                    wait(pool, s3_pool, c.n(POOL3, 3))
                    for t in range(QT):
                        then(pool.tensor_scalar(x1[:, t], a_sb[:, t], mv1[:, t, 0:1], r1[:, t:t + 1],
                                                ALU.subtract, ALU.mult), 3 + t)
                    wait(pool, s3_pool, c.n(POOL3, 5))
                    then(pool.tensor_tensor(x1c[:], x1[:], c1[:].unsqueeze(1).broadcast_to([P, QT, D]), ALU.add), 5)
                    then(pool.tensor_tensor(u1[:, 0], mv1[:, :, 1], r1[:], ALU.mult), 6)
                    wait(pool, s3_pool, c.n(POOL3, 7))
                    then(pool.tensor_tensor(u1[:, 1], u1[:, 0], r1[:], ALU.mult), 7)
                    wait(pool, s3_pool, c.n(POOL3, 8))
                    then(pool.tensor_scalar(u1[:, 2], u1[:, 1], EPS, None, ALU.add, ALU.bypass), 8)
                    wait(pool, s3_pool, c.n(POOL3, 9))
                    then(pool.tensor_tensor(rr1[:], u1[:, 2], half_neg[:], ALU.pow), 9)
                    wait(pool, s3_dve, c.n(DVE3, 13))
                    then(pool.tensor_scalar(ve2[:], mv2[:, :, 1], EPS, None, ALU.add, ALU.bypass), 10)
                    wait(pool, s3_pool, c.n(POOL3, 11))
                    then(pool.tensor_tensor(r2[:], ve2[:], half_neg[:], ALU.pow), 11)
                    wait(pool, s3_pool, c.n(POOL3, 12))
                    for t in range(QT):
                        then(pool.tensor_scalar(z2[:, t], x2[:, c.parity, t], mv2[:, t, 0:1], r2[:, t:t + 1],
                                                ALU.subtract, ALU.mult), 12 + t)
                    wait(pool, x2_out[c.parity], c.uses() - 16)
                    then(pool.tensor_tensor(x12[:, c.parity], x1[:], x2[:, c.parity], ALU.add), 15)

            pairs_of(pool, NB, step)

            def step(i):
                if i.exists():
                    wait(pool, fin_dve, i.n(6, 4))
                    pool.tensor_scalar(ve3[:], mv3[:, :, 1], EPS, None, ALU.add, ALU.bypass).then_inc(fin_pool, 1)
                    wait(pool, fin_pool, i.n(2, 1))
                    pool.tensor_tensor(r3[:], ve3[:], half_neg[:], ALU.pow).then_inc(fin_pool, 1)

            pairs_of(pool, NB, step, before=0, after=0)

        @block.tensor
        def _(pe):
            mm = nc.tensor.matmul
            tr = nc.tensor.transpose

            pe.wait_ge(w_in[0], 80)
            pe.wait_ge(const_ready, 7)
            for n in range(2):
                ins = tr(bank[0][:, n * LAT:(n + 1) * LAT], up_sb[:, n, :], ident[0:LAT, 0:LAT])
            ins.then_inc(set_pe, 1)
            for h in range(HEADS):
                ins = tr(bank[1 + h // 4][:, (h % 4) * P:(h % 4 + 1) * P], wq_sb[:, h, :], ident[:])
            ins.then_inc(set_pe, 1)
            pe.wait_ge(w_in[2], 16 * 8)
            tr(bank[3][:, 0:36], vec_sb[:], ident[0:36, 0:36]).then_inc(set_pe, 1)
            pe.wait_ge(set_act, 2)
            for h in range(HEADS):
                ins = mm(bank[4][:, h * LAT:(h + 1) * LAT], wqT[:, h, :], upT[:, 0, :], start=True, stop=True)
            ins.then_inc(set_pe, 1)
            pe.wait_ge(w_in[1], 16)
            for h in range(HEADS):
                g, r = divmod(h, REP)
                ins = mm(bank[5][LAT * r:LAT * (r + 1), g * P:(g + 1) * P], upT[:, 1, :], wo_sb[:, h, :],
                         start=True, stop=True)
            ins.then_inc(set_pe, 1)
            pe.wait_ge(set_dve, 8)
            mm(bank[6][:, 0:P], bcol[:, 0, :], mix_sb[:], start=True, stop=True)
            mm(bank[6][:, P:P + EXPERTS], bcol[:, 1, :], rw_sb[:], start=True, stop=True).then_inc(set_pe, 1)
            pe.wait_ge(w_in[3], 16)
            for e in range(EXPERTS):
                for f in range(FT):
                    ins = mm(bank[7][:, e * FT + f:e * FT + f + 1], w1_sb[:, e, f * P:(f + 1) * P], vecT[:, 35:36],
                             start=True, stop=True)
            ins.then_inc(set_pe, 1)
            pe.wait_ge(set_act, 3)
            pe.wait_ge(set_dve, SET_DVE)

            def scores(b, h):
                g, p, bk = h // REP, b.parity, SC[h % 2]
                if h == 0:
                    wait(pe, s1_dve, b.n(S1, 2))
                if h % 2 == 0:
                    wait(pe, s1_act, b.n(S1, 4 + h // 2))
                    wait(pe, s1_dve, b.n(S1, 3 + h // 2))
                wait(pe, exp_done, b.n(HB, h - 1))
                for t in range(QT):
                    mm(bk[:, t * T:(t + 1) * T], qs[0:96, p, h, t * P:(t + 1) * P], ks[0:96, p, g, :],
                       start=True, stop=False, skip_group_check=True)
                    ins = mm(bk[:, t * T + t * P:t * T + (t + 1) * P], ident_bf[:], mask_bf[:],
                             start=False, stop=True, skip_group_check=True)
                ins.then_inc(sc_done, 1)

            def transpose_probs(b, h):
                wait(pe, exp_done, b.n(HB, h + 1))
                bb, hh = lag(b, h, 2)
                copied(pe, bb, hh)
                for n in range(3):
                    ins = tr(PT[h % 2][:, n * P:(n + 1) * P], probs[:, h % 4, (0, 1, 2)[n] * P:((0, 1, 2)[n] + 1) * P],
                             ident[:])
                ins.then_inc(pt_done, 1)

            def values(b, h):
                g, r = divmod(h, REP)
                p = b.parity
                copied(pe, b, h)
                if h == 0:
                    wait(pe, s1_dve, b.n(S1, 7))
                    wait(pe, s3_dve, b.n(DVE3, 2 - 2 * DVE3))
                o = YL[p][LAT * r:LAT * (r + 1), :]
                pt = probsT[:, h % 4, :]
                mm(o[:, g * T:(g + 1) * T], v_sb[:, p, 0, g, :], pt[:, 0:T], start=True, stop=False,
                   skip_group_check=True)
                mm(o[:, g * T + P:(g + 1) * T], v_sb[:, p, 1, g, :], pt[:, T:T + P], start=False, stop=True,
                   skip_group_check=True).then_inc(pv_done, 1)

            def s1(c, h):
                if not c.exists() or h > 6:
                    return
                p = c.parity
                if h == 0:
                    wait(pe, s1_dve, c.n(S1))
                    wait(pe, xq_in[p], c.uses())
                    for t in range(QT):
                        ins = tr(PA[:, t * P:(t + 1) * P], xq[:, p, t], ident[:])
                elif h == 6:
                    wait(pe, s1_act, c.n(S1, 7))
                    wait_apart(pe, s1_dve, c.n(S1, 6), S["apart_pe"])
                    for t in range(QT):
                        for g in range(GROUPS):
                            k = (t * GROUPS + g) * LAT
                            ins = tr(PA[:, k:k + LAT], vT[96:128, g, t * P:(t + 1) * P], ident[96:128, 96:128])
                else:
                    hi, lo = (wkv_hi, wkv_lo) if h == 1 else (wq_hi, wq_lo)
                    rows = 4 * LAT if h == 1 else 3 * LAT
                    wait(pe, s1_act, c.n(S1, 1 if h == 1 else h + 1))
                    wait(pe, s1_dve, c.n(S1, h))
                    for n in range(2):
                        j = n if h == 1 else 2 * (h - 2) + n
                        o = PA[0:rows, n * T:(n + 1) * T]
                        w_hi, w_lo = (w[:, j].rearrange("p r l -> p (r l)") for w in (hi, lo))
                        mm(o, w_hi, xT_hi[:], start=True, stop=False)
                        mm(o, w_hi, xT_lo[:], start=False, stop=False)
                        ins = mm(o, w_lo, xT_hi[:], start=False, stop=True)
                ins.then_inc(s1_pe, 1)

            def s3(b, h):
                c = b.shift(-2) if h <= 2 else b.shift(-1)
                if not c.exists():
                    return
                p = c.parity
                if h == 3:
                    wait(pe, s3_pool, c.n(POOL3, 1))
                    wait(pe, s3_dve, c.n(DVE3))
                    for g in range(GROUPS):
                        for t in range(QT):
                            ins = tr(PC[:, (g * QT + t) * P:(g * QT + t + 1) * P],
                                     recb[:, t, g * REP:(g + 1) * REP].rearrange("p h l -> p (h l)"),
                                     ident[:])
                elif h == 4:
                    wait(pe, s3_dve, c.n(DVE3, 2))
                    for t in range(QT):
                        for g in range(GROUPS):
                            ins = mm(PC[:, t * P:(t + 1) * P], ylT[:, g, t * P:(t + 1) * P], wvo[:, g, :],
                                     start=g == 0, stop=g == GROUPS - 1)
                elif h == 6:
                    wait(pe, s3_pool, c.n(POOL3, 5))
                    for t in range(QT):
                        ins = tr(PC[:, t * P:(t + 1) * P], x1[:, t], ident[:])
                elif h == 7:
                    wait(pe, s3_act, c.n(ACT3, 2))
                    for t in range(QT):
                        ins = mm(PC[:, t * P:(t + 1) * P], x1T[:, t * P:(t + 1) * P], m1[:], start=True, stop=True)
                elif h == 1:
                    wait(pe, s3_pool, c.n(POOL3, 14))
                    for t in range(QT):
                        ins = tr(PC[:, t * P:(t + 1) * P], z2[:, t], ident[:])
                elif h == 2:
                    wait(pe, s3_act, c.n(ACT3, 3))
                    for t in range(QT):
                        ins = mm(PC[:, t * EXPERTS:(t + 1) * EXPERTS], z2T[:, p, t * P:(t + 1) * P], rg[:],
                                 start=True, stop=True)
                else:
                    return
                ins.then_inc(s3_pe, 1)

            def step(b):
                for h in range(HEADS):
                    if b.exists():
                        scores(b, h)
                    bb, hh = lag(b, h, 2)
                    if bb.exists():
                        transpose_probs(bb, hh)
                    bb, hh = lag(b, h, 3)
                    if bb.exists():
                        values(bb, hh)
                    s1(b.shift(1), h)
                    s3(b, h)

            pairs_of(pe, NB, step)

            pe.wait_ge(route_dve, 1)
            pe.wait_ge(w_in[4], 32)
            pe.wait_ge(s3_dve, DVE3 * NB)

            def up(b, e):
                p = b.parity
                if e == 0:
                    wait(pe, zin_s[p], b.uses())
                for f in range(FT):
                    if f % 2 == 0:
                        wait(pe, silu_done, b.n(EXPERTS * FT, FT * (e - 2) + f + 2))
                    o = bank[2 * (e % 2) + f // 2]
                    ins = mm(o[:, (f % 2) * T:(f % 2 + 1) * T], w1_sb[:, e, f * P:(f + 1) * P], zin[:, p],
                             start=True, stop=True)
                    if f % 2:
                        ins.then_inc(h_done, 1)

            def down(b, e):
                wait(pe, acc_done, b.n(4 * EXPERTS, 4 * (e - 1)))
                wait(pe, silu_done, b.n(EXPERTS * FT, FT * (e + 1)))
                for t in range(QT):
                    for f in range(FT):
                        ins = mm(bank[4 + e % 2][:, t * P:(t + 1) * P], hT[:, e % 2, f, t * P:(t + 1) * P],
                                 w2_sb[:, e, f, :], start=f == 0, stop=f == FT - 1)
                ins.then_inc(y_done, 1)

            def step(b):
                for e in range(EXPERTS):
                    if b.exists():
                        up(b, e)
                    bb, ee = lag(b, e, 1)
                    if bb.exists():
                        down(bb, ee)
                    if not b.exists():
                        return

            pairs_of(pe, NB, step, before=0, after=1)

        @block.scalar
        def _(act):
            cp = nc.scalar.copy
            act.wait_ge(set_pe, 1)
            cp(upT[:].rearrange("p n l -> p (n l)"), bank[0][:, 0:2 * LAT]).then_inc(set_act, 1)
            act.wait_ge(set_pe, 2)
            cp(wqT[:, 0:4].rearrange("p h k -> p (h k)"), bank[1][:])
            cp(wqT[:, 4:8].rearrange("p h k -> p (h k)"), bank[2][:]).then_inc(set_act, 1)
            act.wait_ge(set_pe, 5)
            cp(wvo[:].rearrange("p g k -> p (g k)"), bank[5][:, 0:2 * P]).then_inc(set_act, 1)
            act.wait_ge(set_dve, SET_DVE)

            def exps(b, h):
                p, bk = b.parity, SC[h % 2]
                wait(act, max_done, b.n(HB, h + 1))
                wait(act, pt_done, b.n(HB, h - 3))
                for t in range(QT):
                    ins = nc.scalar.activation(probs[:, h % 4, t * P:(t + 1 + t) * P], bk[:, t * T:t * T + (t + 1) * P],
                                               ACT.Exp, bias=negm[:, p, t, h:h + 1], accum_out=sums[:, p, t, h:h + 1])
                ins.then_inc(exp_done, 1)

            def copy_probs(b, h):
                if h in ACT_HEADS:
                    wait(act, pt_done, b.n(HB, h + 1))
                    wait(act, pv_done, b.n(HB, h - 3))
                    cp(probsT[:, h % 4, :], PT[h % 2][:, 0:3 * P]).then_inc(pt_act, 1)

            def s1(c, h):
                if not c.exists() or h > 5:
                    return
                p = c.parity
                wait(act, s1_pe, c.n(S1, h + 1))
                if h == 0:
                    cp(xT_hi[:], PA[:, 0:T]).then_inc(s1_act, 1)
                elif h == 1:
                    cp(ks[0:96, p].rearrange("p g t -> p (g t)"), PA[0:96, :]).then_inc(s1_act, 1)
                    cp(vT[96:128].rearrange("p g t -> p (g t)"), PA[96:128, :]).then_inc(s1_act, 1)
                else:
                    j = 2 * (h - 2)
                    cp(qs[0:96, p, j:j + 2].rearrange("p h t -> p (h t)"), PA[0:96, :]).then_inc(s1_act, 1)

            def s3(b, h):
                c = b.shift(-2) if h <= 2 else b.shift(-1)
                if not c.exists():
                    return
                if h == 3:
                    wait(act, s3_pe, c.n(PE3, 1))
                    cp(rs_sb[:].rearrange("p g t -> p (g t)"), PC[:, :]).then_inc(s3_act, 1)
                elif h == 6:
                    wait(act, s3_pe, c.n(PE3, 3))
                    cp(x1T[:], PC[:, 0:T]).then_inc(s3_act, 1)
                elif h == 1:
                    wait(act, s3_pe, c.n(PE3, 5))
                    wait(act, z_out[c.parity], c.uses() - 16 if not isinstance(c.pair, int) else c.uses() - 16)
                    cp(z2T[:, c.parity], PC[:, 0:T]).then_inc(s3_act, 1)

            def step(b):
                for h in range(HEADS):
                    if b.exists():
                        exps(b, h)
                    s1(b.shift(1), h)
                    bb, hh = lag(b, h, 2)
                    if bb.exists():
                        copy_probs(bb, hh)
                    s3(b, h)

            pairs_of(act, NB, step)

            act.wait_ge(route_dve, 2)
            nc.scalar.activation(rt[1][:], rt[0][:], ACT.Exp).then_inc(route_act, 1)

            def step(b):
                for e in range(EXPERTS):
                    for f in range(FT):
                        if f % 2 == 0:
                            wait(act, h_done, b.n(EXPERTS * FT // 2, (e * FT + f) // 2 + 1))
                        if f == 0:
                            wait(act, y_done, b.n(EXPERTS, e - 1))
                        k = e * FT + f
                        nc.scalar.activation(hT[:, e % 2, f, :], bank[2 * (e % 2) + f // 2][:, (f % 2) * T:(f % 2 + 1) * T],
                                             ACT.Silu, bias=b1T[:, k:k + 1]).then_inc(silu_done, 1)

            pairs_of(act, NB, step, before=0, after=0)

        @block.vector
        def _(dve):
            v = nc.vector
            links = [0]

            def link(ins):
                links[0] += 1
                ins.then_inc(set_dve, 1)
                dve.wait_ge(set_dve, links[0])

            dve.wait_ge(set_pe, 3)
            link(v.tensor_copy(vecT[:], bank[3][:, 0:36]))
            link(v.tensor_tensor(mix_sb[:], mix_sb[:], ident[:], ALU.add))
            link(v.tensor_scalar(m1[:], mix_sb[:], vecT[:, 32:33], None, ALU.mult))
            link(v.tensor_scalar(rg[:], rw_sb[:], vecT[:, 34:35], None, ALU.mult))
            link(v.memset(bcol[:], 1.0))
            link(v.tensor_scalar(bcol[:, 0, :], bcol[:, 0, :], vecT[:, 33:34], None, ALU.mult))
            link(v.tensor_scalar(bcol[:, 1, :], bcol[:, 1, :], vecT[:, 35:36], None, ALU.mult))
            link(v.tensor_copy(wkv_hi[:, :, 0:3, :], wkv_sb[:, 0].unsqueeze(2).broadcast_to([P, GROUPS, 3, LAT])))
            v.tensor_copy(wkv_hi[:, :, 3, :], wkv_sb[:, 1])
            link(v.tensor_tensor(wkv_lo[:, :, 0:3, :], wkv_sb[:, 0].unsqueeze(2).broadcast_to([P, GROUPS, 3, LAT]),
                                 wkv_hi[:, :, 0:3, :], ALU.subtract))
            link(v.tensor_tensor(wkv_lo[:, :, 3, :], wkv_sb[:, 1], wkv_hi[:, :, 3, :], ALU.subtract))
            dve.wait_ge(set_pe, 4)
            link(v.tensor_scalar(absq[:].rearrange("p h l -> p (h l)"), bank[4][:, 0:HEADS * LAT], SCALE, None, ALU.mult))
            link(v.tensor_copy(wq_hi[:], absq[:].unsqueeze(2).broadcast_to([P, HEADS, 3, LAT])))
            link(v.tensor_tensor(wq_lo[:], absq[:].unsqueeze(2).broadcast_to([P, HEADS, 3, LAT]), wq_hi[:], ALU.subtract))
            dve.wait_ge(set_pe, 6)
            v.tensor_tensor(c1[:], bank[6][:, 0:P], mixb_bc[:], ALU.add)
            link(v.tensor_copy(rb[:], bank[6][:, P:P + EXPERTS]))
            dve.wait_ge(set_pe, 7)
            v.tensor_tensor(b1T[:], bank[7][:, 0:32], vecT[:, 0:32], ALU.add)
            link(v.tensor_scalar(w1_sb[:], w1_sb[:], vecT[:, 34:35], None, ALU.mult))
            assert links[0] == SET_DVE, links[0]

            def maxes(b, h):
                p, bk = b.parity, SC[h % 2]
                wait(dve, sc_done, b.n(HB, h + 1))
                for t in range(QT):
                    ins = v.tensor_reduce(negm[:, p, t, h:h + 1], bk[:, t * T:t * T + (t + 1) * P], axis=AX.X,
                                          op=ALU.max, negate=True)
                ins.then_inc(max_done, 1)

            def copy_probs(b, h):
                if h not in ACT_HEADS:
                    wait(dve, pt_done, b.n(HB, h + 1))
                    wait(dve, pv_done, b.n(HB, h - 3))
                    v.tensor_copy(probsT[:, h % 4, :], PT[h % 2][:, 0:3 * P]).then_inc(pt_dve, 1)

            def s1(c, h):
                if not c.exists() or h > 6:
                    return
                p = c.parity
                if h == 0:
                    wait(dve, s1_act, c.n(S1, 1))
                    ins = v.tensor_tensor(xT_lo[:], PA[:, 0:T], xT_hi[:], ALU.subtract)
                elif h == 1:
                    wait(dve, s1_act, c.n(S1, 3))
                    k = ks[64:96, p].rearrange("p g t -> p (g t)")
                    ins = v.tensor_tensor(k, PA[64:96, :], k, ALU.subtract)
                elif h == 6:
                    wait(dve, s1_pe, c.n(S1, 7))
                    ins = v.tensor_copy(v_sb[:, p].rearrange("p t g l -> p (t g l)"), PA[:, 0:QT * GROUPS * LAT])
                else:
                    wait(dve, s1_act, c.n(S1, h + 2))
                    j = 2 * (h - 2)
                    q = qs[32:64, p, j:j + 2].rearrange("p h t -> p (h t)")
                    ins = v.tensor_tensor(q, PA[32:64, :], q, ALU.subtract)
                ins.then_inc(s1_dve, 1)

            def s3(b, h):
                c = b.shift(-2) if h <= 2 else b.shift(-1)
                if not c.exists():
                    return
                p = c.parity

                def done(ins):
                    ins.then_inc(s3_dve, 1)

                def stats(src, st, mv, first):
                    wait(dve, s3_dve, c.n(DVE3, first))
                    for t in range(QT):
                        done(v.bn_stats(st[:, t], src[:, t]))
                    wait_apart(dve, s3_dve, c.n(DVE3, first + 2), S["apart_dve"])
                    for t in range(QT):
                        done(v.bn_aggr(mv[:, t], st[:, t]))

                if h == 3:
                    wait(dve, exp_done, c.n(HB, HEADS))
                    done(v.reciprocal(recips[:, p], sums[:, p]))
                elif h == 4:
                    wait(dve, s3_act, c.n(ACT3, 1))
                    wait(dve, pv_done, c.n(HB, HEADS))
                    done(v.tensor_tensor(ylT[:].rearrange("p g t -> p (g t)"), YL[p][:, :],
                                         rs_sb[:].rearrange("p g t -> p (g t)"), ALU.mult))
                elif h == 5:
                    wait(dve, s3_pe, c.n(PE3, 2))
                    wait(dve, xr_in[p], c.uses())
                    done(v.tensor_tensor(a_sb[:], PC[:, 0:T].rearrange("p (t d) -> p t d", t=QT), xr[:, p], ALU.add))
                    stats(a_sb, st1, mv1, 3)
                elif h == 0:
                    wait(dve, s3_pe, c.n(PE3, 4))
                    wait(dve, s3_pool, c.n(POOL3, 10))
                    wait(dve, s3_pool, c.n(POOL3, 15 - POOL3))
                    for t in range(QT):
                        done(v.scalar_tensor_tensor(x2[:, p, t], PC[:, t * P:(t + 1) * P], rr1[:, t:t + 1],
                                                    x1c[:, t], ALU.mult, ALU.add))
                    stats(x2[:, p], st2, mv2, 9)
                elif h == 2:
                    wait(dve, s3_pe, c.n(PE3, 6))
                    tile = c.n(QT)
                    done(v.tensor_tensor(logits[:, bass.ds(tile, QT), :],
                                         PC[:, 0:QT * EXPERTS].rearrange("p (t e) -> p t e", t=QT),
                                         rb[:].unsqueeze(1).broadcast_to([P, QT, EXPERTS]), ALU.add))

            def step(b):
                for h in range(HEADS):
                    if b.exists():
                        maxes(b, h)
                    s1(b.shift(1), h)
                    bb, hh = lag(b, h, 2)
                    if bb.exists():
                        copy_probs(bb, hh)
                    s3(b, h)

            pairs_of(dve, NB, step)

            routed = [0]

            def route(ins):
                routed[0] += 1
                ins.then_inc(route_dve, 1)
                dve.wait_ge(route_dve, routed[0])

            full = [P, TILES, EXPERTS]
            down8 = iota_down[:].unsqueeze(1).broadcast_to(full)
            over = lambda t: t[:].unsqueeze(2).broadcast_to(full)
            dve.wait_ge(s3_dve, DVE3 * NB)
            route(v.tensor_reduce(rs1[0][:], logits[:], axis=AX.X, op=ALU.max))
            route(v.tensor_tensor(rt[0][:], logits[:], over(rs1[0]), ALU.subtract))
            dve.wait_ge(route_act, 1)
            route(v.tensor_reduce(rs1[1][:], rt[1][:], axis=AX.X, op=ALU.add))
            route(v.reciprocal(rs1[2][:], rs1[1][:]))
            route(v.tensor_tensor(rt[1][:], rt[1][:], over(rs1[2]), ALU.mult))
            for n in range(2):
                route(v.tensor_reduce(rs1[0][:], rt[1][:], axis=AX.X, op=ALU.max))
                route(v.tensor_tensor(rt[0][:], rt[1][:], over(rs1[0]), ALU.is_equal))
                route(v.tensor_tensor(rt[0][:], rt[0][:], down8, ALU.mult))
                route(v.tensor_reduce(rs1[3][:], rt[0][:], axis=AX.X, op=ALU.max))
                route(v.tensor_tensor(rt[2 + n][:], down8, over(rs1[3]), ALU.is_equal))
                if n == 0:
                    route(v.tensor_tensor(comb[:], rt[2][:], over(rs1[0]), ALU.mult))
                    route(v.scalar_tensor_tensor(rt[1][:], rt[2][:], -2.0, rt[1][:], ALU.mult, ALU.add))
                else:
                    route(v.tensor_tensor(rt[3][:], rt[3][:], over(rs1[0]), ALU.mult))
                    route(v.tensor_tensor(comb[:], comb[:], rt[3][:], ALU.add))
            dve.wait_ge(w_in[4], 32)

            def step(b):
                if not b.exists():
                    return
                p = b.parity
                for e in range(EXPERTS):
                    for half in range(2):
                        if half:
                            wait(dve, y_done, b.n(EXPERTS, e + 1))
                        elif e == 0:
                            wait(dve, xin_s[p], b.uses())
                            wait(dve, fin_dve, b.n(6))
                        wait(dve, acc_done, b.n(4 * EXPERTS, 4 * e + 2 * half))
                        for t in range(QT):
                            weight = comb[:, bass.ds(b.n(QT, t), 1), e]
                            src = bank[4 + e % 2][:, t * P:(t + 1) * P] if half else b2_bc[:, e, :]
                            base = xin[:, p, t] if e == 0 and not half else acc[:, t]
                            v.scalar_tensor_tensor(acc[:, t], src, weight, base, ALU.mult, ALU.add).then_inc(acc_done, 1)
                wait(dve, acc_done, b.n(4 * EXPERTS, 4 * EXPERTS))
                for t in range(QT):
                    v.bn_stats(st3[:, t], acc[:, t]).then_inc(fin_dve, 1)
                wait_apart(dve, fin_dve, b.n(6, 2), S["apart_dve"])
                for t in range(QT):
                    v.bn_aggr(mv3[:, t], st3[:, t]).then_inc(fin_dve, 1)
                wait(dve, fin_pool, b.n(2, 2))
                wait(dve, o_out[p], b.uses() - 16)
                for t in range(QT):
                    v.tensor_scalar(o_sb[:, p, t], acc[:, t], mv3[:, t, 0:1], r3[:, t:t + 1],
                                    ALU.subtract, ALU.mult).then_inc(fin_dve, 1)

            pairs_of(dve, NB, step, before=0, after=0)


_INS = ['L0_attn_x', 'L0_attn_wq', 'L0_attn_wk_down', 'L0_attn_wv_down', 'L0_attn_wk_up', 'L0_attn_wv_up', 'L0_attn_wo',
        'L0_ffn_g1', 'L0_ffn_be1', 'L0_ffn_mix_w', 'L0_ffn_mix_b', 'L0_ffn_g2', 'L0_ffn_be2', 'L0_ffn_router_w',
        'L0_ffn_w1', 'L0_ffn_b1', 'L0_ffn_w2', 'L0_ffn_b2']


def kernel(**inputs):
    import numpy as np
    import concourse.bacc as bacc
    from concourse.bass_utils import run_bass_kernel_spmd

    nc = bacc.Bacc("TRN2", target_bir_lowering=False, num_devices=1)
    arrays, args = {}, []
    for name in _INS:
        a = np.ascontiguousarray(inputs[name])
        arrays[f"in_{name}"] = a
        args.append(nc.dram_tensor(f"in_{name}", a.shape, mybir.dt.from_np(a.dtype), kind="ExternalInput").ap())
    shape = inputs["L0_attn_x"].shape
    args.append(nc.dram_tensor("out_0", shape, F32, kind="ExternalOutput").ap())
    build(nc, *args)
    r = run_bass_kernel_spmd(nc, [arrays], core_ids=[0])
    return r.results[0]["out_0"]
```

```python
from contextlib import ExitStack

import concourse.bass as bass
from concourse import mybir

F32 = mybir.dt.float32
I32 = mybir.dt.int32
U32 = mybir.dt.uint32
F32R = mybir.dt.float32r
BF16 = mybir.dt.bfloat16
ALU = mybir.AluOpType
ACT = mybir.ActivationFunctionType
AX = mybir.AxisListType

P = 128
EPS = 1e-5
MASKED = -1e30
NOWHERE = 1e6
HEADS = 8
GROUPS = 2
REP = HEADS // GROUPS
LAT = 32
EXPERTS = 8
BLOCK = 2 * P
ROW = 132
ACT_HEADS = (0, 2, 4, 6)
PROJECT_SLOTS = (0, 2, 3, 4, 5, 6, 7)


class Batch:

    def __init__(self, pair, off, count):
        self.pair, self.off, self.count = pair, off, count
        self.parity = off % 2

    def shift(self, d):
        return Batch(self.pair, self.off + d, self.count)

    def pair_shift(self, d):
        if isinstance(self.pair, int):
            return Pair(self.pair + (self.off - self.parity) // 2 + d, self.count // 2)
        return Pair(self.pair + ((self.off - self.parity) // 2 + d), self.count // 2)

    def exists(self):
        return not isinstance(self.pair, int) or 0 <= 2 * self.pair + self.off < self.count

    def n(self, per, k=0):
        if per == 0:
            return k
        return self.pair * (2 * per) + (self.off * per + k)

    def uses(self, per=16):
        return self.pair * per + (self.off // 2 + 1) * per


class Pair:

    def __init__(self, index, count):
        self.index, self.count = index, count

    def exists(self):
        return not isinstance(self.index, int) or 0 <= self.index < self.count

    def n(self, per, k=0):
        return self.index * per + k


def wait(eng, sem, value):
    if not isinstance(value, int) or value > 0:
        eng.wait_ge(sem, value)


def wait_apart(eng, sem, value, apart):
    if not isinstance(value, int) or value > 0:
        eng.wait_ge(sem, value)
        eng.sem_inc(apart)


def pairs_of(eng, batches, step, before=1, after=2, first=2):
    for i in range(-before, 2 * first):
        step(Batch(0, i, batches))
    with eng.Fori(first, batches // 2 - 1) as j:
        step(Batch(j, 0, batches))
        step(Batch(j, 1, batches))
    for i in range(batches - 2, batches + after):
        step(Batch(0, i, batches))


def build(nc, x, wq, wk_down, wv_down, wk_up, wv_up, wo, g1, be1, mix_w, mix_b, g2, be2, router_w, w1, b1, w2, b2, out):
    NB, T, D = x.shape
    F = w1.shape[2]
    FT = F // P
    QT = T // P
    assert D == P and QT == 2 and NB % 2 == 0 and FT == 4
    TILES = NB * QT
    SCALE = float(P) ** -0.5
    HB = HEADS

    x_t = x.rearrange("b (t p) d -> b p t d", p=P)
    out_t = out.rearrange("b (t p) d -> b p t d", p=P)
    TOKENS = NB * T
    REGION = TOKENS + BLOCK
    BLOCKS = 2 * TOKENS // BLOCK + EXPERTS
    SPARE = EXPERTS * REGION
    assert BLOCKS % 2 == 0
    queue_d = nc.dram_tensor("queue_scratch", [SPARE + EXPERTS * BLOCK, ROW], F32).ap()
    y_d = nc.dram_tensor("y_scratch", [2 * TOKENS, D], F32).ap()
    y_t = y_d.rearrange("(k b t p) d -> b p k t d", k=2, b=NB, p=P)

    with ExitStack() as ctx:
        stay, attention = ctx.enter_context(ExitStack()), ExitStack()

        def sb(name, shape, dt=F32, part=None):
            return (part or stay).enter_context(nc.sbuf_tensor(name, shape, dt))

        def sem(name):
            return ctx.enter_context(nc.semaphore(name))

        bank = [ctx.enter_context(nc.psum_tensor(f"bank{i}", [P, 512], F32)) for i in range(8)]
        SC, PT, YL, PA, PC = bank[0:2], bank[2], bank[3], bank[4:6], bank[6:8]

        ident = sb("ident", [P, P])
        ident_bf = sb("ident_bf", [P, P], BF16)
        mask_bf = sb("mask_bf", [P, P], BF16)
        half_neg = sb("half_neg", [P, QT])
        iota_down = sb("iota_down", [P, EXPERTS])
        wq_sb = sb("wq_sb", [P, HEADS, P])
        wo_sb = sb("wo_sb", [P, HEADS, P])
        wkv_sb = sb("wkv_sb", [P, 2, GROUPS, LAT])
        up_sb = sb("up_sb", [LAT, 2, P])
        vec_sb = sb("vec_sb", [36, P])
        upT = sb("upT", [P, 2, LAT])
        wqT = sb("wqT", [P, HEADS, P])
        absq = sb("absq", [P, HEADS, LAT])
        wq_hi = sb("wq_hi", [P, HEADS, 3, LAT], F32R)
        wq_lo = sb("wq_lo", [P, HEADS, 3, LAT], F32R)
        wkv_hi = sb("wkv_hi", [P, GROUPS, 4, LAT], F32R)
        wkv_lo = sb("wkv_lo", [P, GROUPS, 4, LAT], F32R)
        wvo = sb("wvo", [P, GROUPS, P])
        vecT = sb("vecT", [P, 36])
        mix_sb = sb("mix_sb", [P, P])
        mixb_bc = sb("mixb_bc", [P, P])
        m1 = sb("m1", [P, P])
        c1 = sb("c1", [P, P])
        rw_sb = sb("rw_sb", [P, EXPERTS])
        rg = sb("rg", [P, EXPERTS])
        rb = sb("rb", [P, EXPERTS])
        bcol = sb("bcol", [P, 2, P])
        w1_sb = sb("w1_sb", [P, EXPERTS, F + FT])
        w2_sb = sb("w2_sb", [P, EXPERTS, FT, D])
        b2_bc = sb("b2_bc", [P, EXPERTS, D])
        earlier = sb("earlier", [P, P], BF16)
        ones_bf = sb("ones_bf", [P, P], BF16)
        pad_rows = sb("pad_rows", [P, 2, ROW])

        x12 = sb("x12", [P, TILES, D])
        weights = sb("weights", [P, 2, TILES])
        rows_i = sb("rows_i", [1, BLOCKS], I32)
        experts_i = sb("experts_i", [1, BLOCKS], I32)

        xq = sb("xq", [P, 2, QT, D], part=attention)
        xr = sb("xr", [P, 2, QT, D], part=attention)
        xT_hi = sb("xT_hi", [P, T], F32R, part=attention)
        xT_lo = sb("xT_lo", [P, T], F32R, part=attention)
        qs = sb("qs", [P, 2, HEADS, T], F32R, part=attention)
        ks = sb("ks", [P, 2, GROUPS, T], F32R, part=attention)
        vT = sb("vT", [P, GROUPS, T], part=attention)
        v_sb = sb("v_sb", [P, 2, QT, GROUPS, LAT], part=attention)
        negm = sb("negm", [P, 2, QT, HEADS], part=attention)
        sums = sb("sums", [P, 2, QT, HEADS], part=attention)
        recips = sb("recips", [P, QT, HEADS], part=attention)
        recb = sb("recb", [P, QT, HEADS, LAT], part=attention)
        probs = sb("probs", [P, 4, 3 * P], part=attention)
        probsT = sb("probsT", [P, 4, 3 * P], part=attention)
        rs_sb = sb("rs_sb", [P, GROUPS, T], part=attention)
        ylT = sb("ylT", [P, GROUPS, T], part=attention)

        a_sb = sb("a_sb", [P, QT, D], part=attention)
        st1 = sb("st1", [P, QT, 6], part=attention)
        mv1 = sb("mv1", [P, QT, 2], part=attention)
        ve1 = sb("ve1", [P, QT], part=attention)
        r1 = sb("r1", [P, QT], part=attention)
        u1 = sb("u1", [P, 3, QT], part=attention)
        rr1 = sb("rr1", [P, QT], part=attention)
        x1 = sb("x1", [P, QT, D], part=attention)
        x1c = sb("x1c", [P, QT, D], part=attention)
        x1T = sb("x1T", [P, T], part=attention)
        x2 = sb("x2", [P, QT, D], part=attention)
        st2 = sb("st2", [P, QT, 6], part=attention)
        mv2 = sb("mv2", [P, QT, 2], part=attention)
        ve2 = sb("ve2", [P, QT], part=attention)
        r2 = sb("r2", [P, QT], part=attention)
        z2_all = sb("z2_all", [P, TILES, D], part=attention)
        z2 = sb("z2", [P, QT, D], part=attention)
        z2T = sb("z2T", [P, T], part=attention)
        logits = sb("logits", [P, 2, QT, EXPERTS], part=attention)

        RT = 2 * QT
        small = [P, RT, EXPERTS]
        shifted = sb("shifted", small, part=attention)
        expd = sb("expd", small, part=attention)
        gate = sb("gate", small, part=attention)
        equal = sb("equal", small, part=attention)
        first_hot = sb("first_hot", small, part=attention)
        second_hot = sb("second_hot", small, part=attention)
        both_hot = sb("both_hot", small, BF16, part=attention)
        top_max = sb("top_max", [P, RT], part=attention)
        top_sum = sb("top_sum", [P, RT], part=attention)
        top_rec = sb("top_rec", [P, RT], part=attention)
        top_w = sb("top_w", [P, 2, RT], part=attention)
        rank0 = sb("rank0", [P, RT], part=attention)
        rank1 = sb("rank1", [P, RT], part=attention)
        ranks = sb("ranks", [P, 2, RT, EXPERTS], part=attention)
        counts = sb("counts", [P, EXPERTS, RT], part=attention)
        totals = sb("totals", [P, EXPERTS, RT], part=attention)
        keep = sb("keep", [P, EXPERTS, RT], part=attention)
        base = sb("base", [P, EXPERTS], part=attention)
        place = sb("place", small, part=attention)
        picked = sb("picked", small, part=attention)
        slots = sb("slots", [P, 2, RT], U32, part=attention)
        first_expert = sb("first_expert", [P, RT], part=attention)
        stage = sb("stage", [P, RT, ROW], part=attention)

        steps_of = sb("steps_of", [P, TOKENS // BLOCK], part=attention)
        block_no = sb("block_no", [P, BLOCKS], part=attention)
        region = sb("region", [P, EXPERTS], part=attention)
        amount = sb("amount", [P, EXPERTS], part=attention)
        filled = sb("filled", [P, EXPERTS, TOKENS // BLOCK], part=attention)
        n_blocks = sb("n_blocks", [P, EXPERTS], part=attention)
        ones8 = sb("ones8", [P, EXPERTS], part=attention)
        ends = sb("ends", [P, EXPERTS], part=attention)
        past = sb("past", [P, BLOCKS, EXPERTS], part=attention)
        past_n = sb("past_n", [P, BLOCKS, EXPERTS], part=attention)
        block_expert = sb("block_expert", [P, BLOCKS], part=attention)
        block_start = sb("block_start", [P, BLOCKS], part=attention)
        block_row = sb("block_row", [P, BLOCKS], part=attention)
        pads_i = sb("pads_i", [1, EXPERTS], I32, part=attention)

        attention.close()
        xb = sb("xb", [P, 2, 2, ROW])
        zT = sb("zT", [P, 2, BLOCK])
        w1_cur = sb("w1_cur", [P, 2, F + FT])
        hT = sb("hT", [P, 2, FT, BLOCK])
        other = sb("other", [P, 2])
        dest = sb("dest", [P, 2, 2], U32)
        yb = sb("yb", [P, 2, 2, D])
        yv = sb("yv", [P, 2, 2, QT, D])
        acc1 = sb("acc1", [P, QT, D])
        acc = sb("acc", [P, 2, QT, D])
        st3 = sb("st3", [P, QT, 6])
        mv3 = sb("mv3", [P, 2, QT, 2])
        ve3 = sb("ve3", [P, QT])
        r3 = sb("r3", [P, 2, QT])
        mr3 = sb("mr3", [P, QT])
        nb3 = sb("nb3", [P, 2, QT])
        o_sb = sb("o_sb", [P, 2, QT, D])

        names = ("w_in0 w_in1 w_in2 w_in3 w_in4 const_ready set_pe set_act set_dve xq_in0 xq_in1 xr_in0 xr_in1 "
                 "s1_pe s1_act s1_dve sc_done max_done exp_done pt_done pt_act pt_dve pv_done "
                 "a_pe a_act a_dve a_pool b_pe b_act b_dve b_pool r_pe r_act r_dve r_pool queued pads_sent "
                 "plan_dve apart_pool apart_pe apart_dve apart_sp xb_in0 xb_in1 t_done zt_done w1_moved up_done silu_done "
                 "down_done y_read dest_done y_sent0 y_sent1 yv_in0 yv_in1 fin_dve fin_pool fin_act o_out0 o_out1").split()
        S = {n: sem(n) for n in names}
        xq_in = [S["xq_in0"], S["xq_in1"]]
        xr_in = [S["xr_in0"], S["xr_in1"]]
        xb_in = [S["xb_in0"], S["xb_in1"]]
        y_sent = [S["y_sent0"], S["y_sent1"]]
        yv_in = [S["yv_in0"], S["yv_in1"]]
        o_out = [S["o_out0"], S["o_out1"]]
        w_in = [S[f"w_in{i}"] for i in range(5)]
        const_ready, set_pe, set_act, set_dve = (S[n] for n in "const_ready set_pe set_act set_dve".split())
        s1_pe, s1_act, s1_dve = S["s1_pe"], S["s1_act"], S["s1_dve"]
        sc_done, max_done, exp_done, pt_done, pv_done = (S[n] for n in "sc_done max_done exp_done pt_done pv_done".split())
        pt_act, pt_dve = S["pt_act"], S["pt_dve"]
        a_pe, a_act, a_dve, a_pool = (S[n] for n in "a_pe a_act a_dve a_pool".split())
        b_pe, b_act, b_dve, b_pool = (S[n] for n in "b_pe b_act b_dve b_pool".split())
        r_pe, r_act, r_dve, r_pool = (S[n] for n in "r_pe r_act r_dve r_pool".split())
        queued, pads_sent, plan_dve = S["queued"], S["pads_sent"], S["plan_dve"]
        t_done, zt_done, w1_moved, up_done = (S[n] for n in "t_done zt_done w1_moved up_done".split())
        silu_done, down_done, y_read, dest_done = (S[n] for n in "silu_done down_done y_read dest_done".split())
        fin_dve, fin_pool, fin_act = (S[n] for n in "fin_dve fin_pool fin_act".split())

        NA = len(ACT_HEADS)
        ND = HEADS - NA
        S1 = 7
        A_PE, A_ACT, A_DVE, A_POOL = 3, 2, 7, 9
        B_PE, B_ACT, B_DVE, B_POOL = 3, 2, 9, 4
        R_DVE, R_POOL = 30, 3
        PLAN = 15
        SET_DVE = 17
        CONSTS = 19
        LAG = dict(after=6, first=4)

        def copied(eng, b, h):
            if h in ACT_HEADS:
                wait(eng, pt_act, b.n(NA, sum(k <= h for k in ACT_HEADS)))
            else:
                wait(eng, pt_dve, b.n(ND, sum(k <= h and k not in ACT_HEADS for k in range(HEADS))))

        def lag(b, h, d):
            return (b, h - d) if h >= d else (b.shift(-1), h - d + HEADS)

        block = ctx.enter_context(nc.Block())

        @block.sync
        def _(sp):
            sp.dma_start(wq_sb[:], wq.rearrange("d (h k) -> d h k", h=HEADS)).then_inc(w_in[0], 16)
            sp.dma_start(up_sb[:, 0, :], wk_up).then_inc(w_in[0], 16)
            sp.dma_start(up_sb[:, 1, :], wv_up).then_inc(w_in[0], 16)
            sp.dma_start(wkv_sb[:, 0], wk_down.rearrange("d (g l) -> d g l", g=GROUPS)).then_inc(w_in[0], 16)
            sp.dma_start(wkv_sb[:, 1], wv_down.rearrange("d (g l) -> d g l", g=GROUPS)).then_inc(w_in[0], 16)
            sp.dma_start(wo_sb[:], wo.rearrange("(h k) d -> k h d", h=HEADS)).then_inc(w_in[1], 16)
            sp.dma_start(vec_sb[0:32, :], b1.rearrange("e (f p) -> (e f) p", p=P)).then_inc(w_in[2], 16)
            for n, v in enumerate((g1, be1, g2, be2)):
                sp.dma_start(vec_sb[32 + n:33 + n, :], v.rearrange("(a d) -> a d", a=1)).then_inc(w_in[2], 16)
            sp.dma_start(mix_sb[:], mix_w).then_inc(w_in[2], 16)
            sp.dma_start(mixb_bc[:], mix_b.partition_broadcast(P)).then_inc(w_in[2], 16)
            sp.dma_start(rw_sb[:], router_w).then_inc(w_in[2], 16)
            sp.dma_start(w1_sb[:, :, 0:F], w1.rearrange("e d f -> d e f")).then_inc(w_in[3], 16)
            sp.dma_start(w2_sb[:], w2.rearrange("e (f p) d -> p e f d", p=P)).then_inc(w_in[4], 16)
            sp.dma_start(b2_bc[:], b2.partition_broadcast(P)).then_inc(w_in[4], 16)

            def step(i):
                c, p = i.shift(1), i.shift(1).parity
                if c.exists():
                    wait(sp, s1_pe, c.n(S1, 1 - 2 * S1))
                    sp.dma_start(xq[:, p], x_t[dyn(c)]).then_inc(xq_in[p], 16)
                c, p = i, i.parity
                if c.exists():
                    wait(sp, a_dve, c.n(A_DVE, 3 - 2 * A_DVE))
                    sp.dma_start(xr[:, p], x_t[dyn(c)]).then_inc(xr_in[p], 16)

            def dyn(c):
                return c.n(1)

            sp.wait_ge(const_ready, CONSTS)
            for n in range(EXPERTS):
                sp.dma_start(queue_d[SPARE + n * BLOCK:SPARE + (n + 1) * BLOCK, :].rearrange("(m p) d -> p m d", p=P),
                             pad_rows[:]).then_inc(pads_sent, 16)
            pairs_of(sp, NB, step, **LAG)
            sp.wait_ge(plan_dve, 1)
            for e in range(EXPERTS):
                end = sp.value_load(pads_i[0:1, e:e + 1], min_val=0, max_val=SPARE - BLOCK)
                sp.dma_start(queue_d[bass.ds(end, BLOCK), :].rearrange("(m p) d -> p m d", p=P),
                             pad_rows[:]).then_inc(pads_sent, 16)
            sp.wait_ge(pads_sent, 2 * EXPERTS * 16)
            sp.wait_ge(queued, 16 * 2 * TILES)
            sp.wait_ge(plan_dve, PLAN)

            def step(i):
                c = i.shift(2)
                if c.exists():
                    p = c.parity
                    row = sp.value_load(rows_i[0:1, bass.ds(c.n(1), 1)], min_val=0, max_val=SPARE + (EXPERTS - 1) * BLOCK)
                    wait_apart(sp, t_done, c.n(1, -1), S["apart_sp"])
                    wait_apart(sp, dest_done, c.n(2, -2), S["apart_sp"])
                    sp.dma_start(xb[:, p], queue_d[bass.ds(row, BLOCK), :].rearrange("(m p) d -> p m d", p=P)
                                 ).then_inc(xb_in[p], 16)

            pairs_of(sp, BLOCKS, step, before=2, after=0)
            for p in range(2):
                sp.wait_ge(y_sent[p], 32 * BLOCKS // 2)

            def step(i):
                c, p = i.shift(2), i.shift(2).parity
                if c.exists():
                    wait(sp, fin_dve, c.n(8, 4 - 16))
                    for k in range(2):
                        sp.dma_start(yv[:, p, k], y_t[dyn(c)][:, k]).then_inc(yv_in[p], 16)
                c, p = i.shift(-1), i.shift(-1).parity
                if c.exists():
                    wait(sp, fin_act, c.n(2, 2))
                    sp.dma_start(out_t[dyn(c)], o_sb[:, p]).then_inc(o_out[p], 16)

            pairs_of(sp, NB, step, before=2, after=1)
            for p in range(2):
                sp.wait_ge(o_out[p], 16 * NB // 2)

        @block.gpsimd
        def _(pool):
            def const(ins):
                ins.then_inc(const_ready, 1)

            def ramp(t, pattern, start=0, by_row=0):
                const(pool.iota(t, pattern=pattern, base=start, channel_multiplier=by_row,
                                allow_small_or_imprecise_dtypes=True))

            const(pool.memset(ident[:], 0.0))
            const(pool.memset(mask_bf[:], 0.0))
            const(pool.memset(half_neg[:], -0.5))
            ramp(iota_down[:], [[-1, EXPERTS]], start=EXPERTS)
            const(pool.memset(earlier[:], 1.0))
            const(pool.memset(ones_bf[:], 1.0))
            const(pool.memset(pad_rows[:], 0.0))
            const(pool.memset(keep[:], 1.0))
            const(pool.memset(ones8[:], 1.0))
            ramp(region[:], [[REGION, EXPERTS]])
            ramp(steps_of[:], [[BLOCK, TOKENS // BLOCK]])
            ramp(block_no[:], [[1, BLOCKS]])
            const(pool.memset(stage[:], 0.0))
            pool.wait_ge(const_ready, 13)
            const(pool.affine_select(out=ident[:], in_=ident[:], compare_op=ALU.not_equal, fill=1.0,
                                     base=0, pattern=[[-1, P]], channel_multiplier=1))
            const(pool.affine_select(out=mask_bf[:], in_=mask_bf[:], compare_op=ALU.is_ge, fill=MASKED,
                                     base=0, pattern=[[-1, P]], channel_multiplier=1))
            const(pool.affine_select(out=earlier[:], in_=earlier[:], compare_op=ALU.is_ge, fill=0.0,
                                     base=-1, pattern=[[1, P]], channel_multiplier=-1))
            const(pool.memset(pad_rows[:, :, D:D + 1], NOWHERE))
            ramp(stage[:, :, D], [[P, RT]], start=-RT * P, by_row=1)
            pool.wait_ge(const_ready, 18)
            pool.tensor_copy(ident_bf[:], ident[:]).then_inc(const_ready, 1)

            def wait(eng, sem, value):
                wait_apart(eng, sem, value, S["apart_pool"])

            def fetch(q):
                if not q.exists():
                    return
                wait(pool, queued, q.n(16 * 2 * RT))
                wait(pool, r_dve, q.n(R_DVE, R_DVE))
                pool.tensor_copy(stage[:, :, 0:D], z2_all[:, bass.ds(q.n(RT), RT), :]).then_inc(r_pool, 1)
                pool.tensor_scalar(stage[:, :, D], stage[:, :, D], float(RT * P), None, ALU.add,
                                   ALU.bypass).then_inc(r_pool, 1)
                pool.tensor_copy(stage[:, :, D + 1], first_expert[:]).then_inc(r_pool, 1)
                wait(pool, r_pool, q.n(R_POOL, R_POOL))

            def enqueue(q, which):
                if not q.exists():
                    return
                for n in which:
                    k, t = divmod(n, RT)
                    pool.indirect_dma_start(
                        out=queue_d, out_offset=bass.IndirectOffsetOnAxis(ap=slots[:, k, t:t + 1], axis=0),
                        in_=stage[:, t, :], in_offset=None, bounds_check=SPARE - 1, oob_is_err=False,
                    ).then_inc(queued, 16)

            def step(i):
                even = i.parity == 0
                q = i.pair_shift(-3)
                if even:
                    fetch(q)
                c = i.shift(-2)
                if c.exists():
                    wait(pool, b_dve, c.n(B_DVE, 6))
                    pool.tensor_scalar(ve2[:], mv2[:, :, 1], EPS, None, ALU.add, ALU.bypass).then_inc(b_pool, 1)
                    wait(pool, b_pool, c.n(B_POOL, 1))
                    pool.tensor_tensor(r2[:], ve2[:], half_neg[:], ALU.pow).then_inc(b_pool, 1)
                    pool.tensor_tensor(x12[:, bass.ds(c.n(QT), QT), :], x1[:], x2[:], ALU.add).then_inc(b_pool, 1)
                    wait(pool, b_dve, c.n(B_DVE, 8))
                    pool.tensor_copy(z2_all[:, bass.ds(c.n(QT), QT), :], z2[:]).then_inc(b_pool, 1)
                enqueue(q, range(0, 3) if even else range(6, 8))
                c = i.shift(-1)
                if c.exists():
                    wait(pool, a_dve, c.n(A_DVE, 7))
                    pool.tensor_scalar(ve1[:], mv1[:, :, 1], EPS, None, ALU.add, ALU.bypass).then_inc(a_pool, 1)
                    wait(pool, a_pool, c.n(A_POOL, 1))
                    pool.tensor_tensor(r1[:], ve1[:], half_neg[:], ALU.pow).then_inc(a_pool, 1)
                    wait(pool, a_pool, c.n(A_POOL, 2))
                    wait(pool, b_pool, c.n(B_POOL))
                    for t in range(QT):
                        pool.tensor_scalar(x1[:, t], a_sb[:, t], mv1[:, t, 0:1], r1[:, t:t + 1],
                                           ALU.subtract, ALU.mult).then_inc(a_pool, 1)
                    wait(pool, a_pool, c.n(A_POOL, 4))
                    pool.tensor_tensor(x1c[:], x1[:], c1[:].unsqueeze(1).broadcast_to([P, QT, D]),
                                       ALU.add).then_inc(a_pool, 1)
                    pool.tensor_tensor(u1[:, 0], mv1[:, :, 1], r1[:], ALU.mult).then_inc(a_pool, 1)
                    wait(pool, a_pool, c.n(A_POOL, 6))
                    pool.tensor_tensor(u1[:, 1], u1[:, 0], r1[:], ALU.mult).then_inc(a_pool, 1)
                    wait(pool, a_pool, c.n(A_POOL, 7))
                    pool.tensor_scalar(u1[:, 2], u1[:, 1], EPS, None, ALU.add, ALU.bypass).then_inc(a_pool, 1)
                    wait(pool, a_pool, c.n(A_POOL, 8))
                    pool.tensor_tensor(rr1[:], u1[:, 2], half_neg[:], ALU.pow).then_inc(a_pool, 1)

                if even:
                    enqueue(q, range(3, 6))

            pairs_of(pool, NB, step, **LAG)

            def step(i):
                c, p = i, i.parity
                if c.exists():
                    wait(pool, y_read, c.n(1, 1))
                    wait(pool, dest_done, c.n(2, 2))
                    for m in range(2):
                        pool.indirect_dma_start(
                            out=y_d, out_offset=bass.IndirectOffsetOnAxis(ap=dest[:, p, m:m + 1], axis=0),
                            in_=yb[:, p, m, :], in_offset=None, bounds_check=2 * TOKENS - 1, oob_is_err=False,
                        ).then_inc(y_sent[p], 16)

            pairs_of(pool, BLOCKS, step, before=0, after=0)

            def step(i):
                c, p = i, i.parity
                if c.exists():
                    wait(pool, fin_dve, c.n(8, 8))
                    wait(pool, fin_act, c.n(2, -2))
                    pool.tensor_scalar(ve3[:], mv3[:, p, :, 1], EPS, None, ALU.add, ALU.bypass).then_inc(fin_pool, 1)
                    wait(pool, fin_pool, c.n(4, 1))
                    pool.tensor_tensor(r3[:, p], ve3[:], half_neg[:], ALU.pow).then_inc(fin_pool, 1)
                    wait(pool, fin_pool, c.n(4, 2))
                    pool.tensor_tensor(mr3[:], mv3[:, p, :, 0], r3[:, p], ALU.mult).then_inc(fin_pool, 1)
                    wait(pool, fin_pool, c.n(4, 3))
                    pool.tensor_scalar(nb3[:, p], mr3[:], -1.0, None, ALU.mult, ALU.bypass).then_inc(fin_pool, 1)

            pairs_of(pool, NB, step, before=0, after=0)

        @block.tensor
        def _(pe):
            mm = nc.tensor.matmul
            tr = nc.tensor.transpose

            pe.wait_ge(w_in[0], 80)
            pe.wait_ge(const_ready, CONSTS)
            for n in range(2):
                ins = tr(bank[0][:, n * LAT:(n + 1) * LAT], up_sb[:, n, :], ident[0:LAT, 0:LAT])
            ins.then_inc(set_pe, 1)
            for h in range(HEADS):
                ins = tr(bank[1 + h // 4][:, (h % 4) * P:(h % 4 + 1) * P], wq_sb[:, h, :], ident[:])
            ins.then_inc(set_pe, 1)
            pe.wait_ge(w_in[2], 16 * 8)
            tr(bank[3][:, 0:36], vec_sb[:], ident[0:36, 0:36]).then_inc(set_pe, 1)
            pe.wait_ge(set_act, 2)
            for h in range(HEADS):
                ins = mm(bank[4][:, h * LAT:(h + 1) * LAT], wqT[:, h, :], upT[:, 0, :], start=True, stop=True)
            ins.then_inc(set_pe, 1)
            pe.wait_ge(w_in[1], 16)
            for h in range(HEADS):
                g, r = divmod(h, REP)
                ins = mm(bank[5][LAT * r:LAT * (r + 1), g * P:(g + 1) * P], upT[:, 1, :], wo_sb[:, h, :],
                         start=True, stop=True)
            ins.then_inc(set_pe, 1)
            pe.wait_ge(set_dve, 8)
            mm(bank[6][:, 0:P], bcol[:, 0, :], mix_sb[:], start=True, stop=True)
            mm(bank[6][:, P:P + EXPERTS], bcol[:, 1, :], rw_sb[:], start=True, stop=True).then_inc(set_pe, 1)
            pe.wait_ge(w_in[3], 16)
            for e in range(EXPERTS):
                for f in range(FT):
                    ins = mm(bank[7][:, e * FT + f:e * FT + f + 1], w1_sb[:, e, f * P:(f + 1) * P], vecT[:, 35:36],
                             start=True, stop=True)
            ins.then_inc(set_pe, 1)
            pe.wait_ge(set_act, 3)
            pe.wait_ge(set_dve, SET_DVE)

            def scores(b, h):
                g, p, bk = h // REP, b.parity, SC[h % 2]
                if h == 0:
                    wait(pe, s1_dve, b.n(S1, 2))
                if h % 2 == 0:
                    wait(pe, s1_act, b.n(S1, 4 + h // 2))
                    wait(pe, s1_dve, b.n(S1, 3 + h // 2))
                wait(pe, exp_done, b.n(HB, h - 1))
                for t in range(QT):
                    mm(bk[:, t * T:(t + 1) * T], qs[0:96, p, h, t * P:(t + 1) * P], ks[0:96, p, g, :],
                       start=True, stop=False, skip_group_check=True)
                    ins = mm(bk[:, t * T + t * P:t * T + (t + 1) * P], ident_bf[:], mask_bf[:],
                             start=False, stop=True, skip_group_check=True)
                ins.then_inc(sc_done, 1)

            def transpose_probs(b, h):
                wait(pe, exp_done, b.n(HB, h + 1))
                copied(pe, *lag(b, h, 1))
                for n in range(3):
                    ins = tr(PT[:, n * P:(n + 1) * P], probs[:, h % 4, n * P:(n + 1) * P], ident[:])
                ins.then_inc(pt_done, 1)

            def values(b, h):
                g, r = divmod(h, REP)
                p = b.parity
                copied(pe, b, h)
                if h == 0:
                    wait(pe, s1_dve, b.n(S1, 7))
                    wait(pe, a_dve, b.n(A_DVE, 2 - A_DVE))
                o = YL[LAT * r:LAT * (r + 1), :]
                pt = probsT[:, h % 4, :]
                mm(o[:, g * T:(g + 1) * T], v_sb[:, p, 0, g, :], pt[:, 0:T], start=True, stop=False,
                   skip_group_check=True)
                mm(o[:, g * T + P:(g + 1) * T], v_sb[:, p, 1, g, :], pt[:, T:T + P], start=False, stop=True,
                   skip_group_check=True).then_inc(pv_done, 1)

            def s1(c, slot):
                if not c.exists() or slot not in PROJECT_SLOTS:
                    return
                k = PROJECT_SLOTS.index(slot)
                p, pa = c.parity, PA[(c.parity + k) % 2]
                wait(pe, s1_dve, c.n(S1, k - 1))
                if k == 0:
                    wait(pe, xq_in[p], c.uses())
                    for t in range(QT):
                        ins = tr(pa[:, t * P:(t + 1) * P], xq[:, p, t], ident[:])
                elif k == 6:
                    wait_apart(pe, s1_act, c.n(S1, 3), S["apart_pe"])
                    for t in range(QT):
                        for g in range(GROUPS):
                            o = (t * GROUPS + g) * LAT
                            ins = tr(pa[:, o:o + LAT], vT[96:128, g, t * P:(t + 1) * P], ident[96:128, 96:128])
                else:
                    hi, lo = (wkv_hi, wkv_lo) if k == 1 else (wq_hi, wq_lo)
                    rows = 4 * LAT if k == 1 else 3 * LAT
                    wait(pe, s1_dve, c.n(S1, 1))
                    for n in range(2):
                        j = n if k == 1 else 2 * (k - 2) + n
                        o = pa[0:rows, n * T:(n + 1) * T]
                        w_hi, w_lo = (w[:, j].rearrange("p r l -> p (r l)") for w in (hi, lo))
                        mm(o, w_hi, xT_hi[:], start=True, stop=False)
                        mm(o, w_hi, xT_lo[:], start=False, stop=False)
                        ins = mm(o, w_lo, xT_hi[:], start=False, stop=True)
                ins.then_inc(s1_pe, 1)

            def after(b, slot):
                c = b.shift(-1)
                if c.exists() and slot == 1:
                    wait(pe, a_act, c.n(A_ACT, 1))
                    wait(pe, b_act, c.n(B_ACT, 1 - B_ACT))
                    for g in range(GROUPS):
                        for t in range(QT):
                            ins = tr(PC[0][:, (g * QT + t) * P:(g * QT + t + 1) * P],
                                     recb[:, t, g * REP:(g + 1) * REP].rearrange("p h l -> p (h l)"), ident[:])
                    ins.then_inc(a_pe, 1)
                if c.exists() and slot == 4:
                    wait(pe, a_dve, c.n(A_DVE, 2))
                    for t in range(QT):
                        for g in range(GROUPS):
                            ins = mm(PC[0][:, t * P:(t + 1) * P], ylT[:, g, t * P:(t + 1) * P], wvo[:, g, :],
                                     start=g == 0, stop=g == GROUPS - 1)
                    ins.then_inc(a_pe, 1)
                if c.exists() and slot == 7:
                    wait(pe, a_pool, c.n(A_POOL, 4))
                    for t in range(QT):
                        ins = tr(PC[0][:, t * P:(t + 1) * P], x1[:, t], ident[:])
                    ins.then_inc(a_pe, 1)
                c = b.shift(-2)
                if c.exists() and slot == 1:
                    wait(pe, b_dve, c.n(B_DVE))
                    wait(pe, b_act, c.n(B_ACT, 1))
                    for t in range(QT):
                        ins = mm(PC[1][:, t * P:(t + 1) * P], x1T[:, t * P:(t + 1) * P], m1[:], start=True, stop=True)
                    ins.then_inc(b_pe, 1)
                q = b.pair_shift(-2)
                if q.exists() and b.parity == 1 and slot == 3:
                    wait(pe, r_dve, q.n(R_DVE, 17))
                    wait(pe, b_dve, b.shift(-2).n(B_DVE, 2) if b.shift(-2).exists() else 0)
                    hot = both_hot[:].rearrange("p t e -> p (t e)")
                    n = RT * EXPERTS
                    mm(PC[1][:, 0:n], earlier[:], hot, start=True, stop=True)
                    mm(PC[1][:, n:2 * n], ones_bf[:], hot, start=True, stop=True).then_inc(r_pe, 1)
                if c.exists() and slot == 4:
                    wait(pe, b_dve, c.n(B_DVE, 8))
                    q = b.pair_shift(-2)
                    wait(pe, r_dve, (q.n(R_DVE, 18) if b.parity == 1 else q.n(R_DVE, 18 - R_DVE)) if q.exists() or
                         b.parity == 0 else 0)
                    for t in range(QT):
                        ins = tr(PC[1][:, t * P:(t + 1) * P], z2[:, t], ident[:])
                    ins.then_inc(b_pe, 1)
                if c.exists() and slot == 6:
                    wait(pe, b_act, c.n(B_ACT, 2))
                    for t in range(QT):
                        ins = mm(PC[1][:, t * EXPERTS:(t + 1) * EXPERTS], z2T[:, t * P:(t + 1) * P], rg[:],
                                 start=True, stop=True)
                    ins.then_inc(b_pe, 1)

            def step(b):
                for h in range(HEADS):
                    if b.exists():
                        scores(b, h)
                    bb, hh = lag(b, h, 2)
                    if bb.exists():
                        transpose_probs(bb, hh)
                    s1(b.shift(1), h)
                    after(b, h)
                    bb, hh = lag(b, h, 3)
                    if bb.exists():
                        values(bb, hh)

            pairs_of(pe, NB, step, **LAG)

            pe.wait_ge(w_in[4], 32)
            pe.wait_ge(plan_dve, PLAN)

            def expert_of(eng, c):
                return eng.value_load(experts_i[0:1, bass.ds(c.n(1), 1)], min_val=0, max_val=EXPERTS - 1)

            def rows_to_columns(c):
                p = c.parity
                wait(pe, xb_in[p], c.uses())
                wait(pe, zt_done, c.n(1, -1))
                for m in range(2):
                    ins = tr(bank[6 + p][:, m * P:(m + 1) * P], xb[:, p, m, 0:D], ident[:])
                ins.then_inc(t_done, 1)

            def up(c):
                p = c.parity
                wait(pe, zt_done, c.n(1, 1))
                wait(pe, w1_moved, c.n(1, 1))
                for f in range(FT):
                    if f % 2 == 0:
                        wait(pe, silu_done, c.n(FT, f + 2 - 2 * FT))
                    ins = mm(bank[2 * p + f // 2][:, (f % 2) * BLOCK:(f % 2 + 1) * BLOCK], w1_cur[:, p, f * P:(f + 1) * P],
                             zT[:, p], start=True, stop=True)
                    if f % 2:
                        ins.then_inc(up_done, 1)

            def down(c):
                p = c.parity
                e = expert_of(pe, c)
                wait(pe, silu_done, c.n(FT, FT))
                wait(pe, y_read, c.n(1, -1))
                for m in range(2):
                    for f in range(FT):
                        ins = mm(bank[4 + p][:, m * P:(m + 1) * P], hT[:, p, f, m * P:(m + 1) * P],
                                 w2_sb[:, bass.ds(e, 1), f, :].rearrange("p e d -> p (e d)"),
                                 start=f == 0, stop=f == FT - 1)
                ins.then_inc(down_done, 1)

            def step(i):
                if i.shift(1).exists():
                    rows_to_columns(i.shift(1))
                if i.exists():
                    up(i)
                if i.shift(-1).exists():
                    down(i.shift(-1))

            pairs_of(pe, BLOCKS, step, before=1, after=1)

        @block.scalar
        def _(act):
            cp = nc.scalar.copy
            act.wait_ge(set_pe, 1)
            cp(upT[:].rearrange("p n l -> p (n l)"), bank[0][:, 0:2 * LAT]).then_inc(set_act, 1)
            act.wait_ge(set_pe, 2)
            cp(wqT[:, 0:4].rearrange("p h k -> p (h k)"), bank[1][:])
            cp(wqT[:, 4:8].rearrange("p h k -> p (h k)"), bank[2][:]).then_inc(set_act, 1)
            act.wait_ge(set_pe, 5)
            cp(wvo[:].rearrange("p g k -> p (g k)"), bank[5][:, 0:2 * P]).then_inc(set_act, 1)
            act.wait_ge(set_dve, SET_DVE)

            def exps(b, h):
                p, bk = b.parity, SC[h % 2]
                wait(act, max_done, b.n(HB, h + 1))
                wait(act, pt_done, b.n(HB, h - 3))
                for t in range(QT):
                    ins = nc.scalar.activation(probs[:, h % 4, t * P:(t + 1 + t) * P], bk[:, t * T:t * T + (t + 1) * P],
                                               ACT.Exp, bias=negm[:, p, t, h:h + 1], accum_out=sums[:, p, t, h:h + 1])
                ins.then_inc(exp_done, 1)

            def copy_probs(b, h):
                if h in ACT_HEADS:
                    wait(act, pt_done, b.n(HB, h + 1))
                    wait(act, pv_done, b.n(HB, h - 3))
                    cp(probsT[:, h % 4, :], PT[:, 0:3 * P]).then_inc(pt_act, 1)

            def s1(c, slot):
                if not c.exists() or slot not in PROJECT_SLOTS:
                    return
                k = PROJECT_SLOTS.index(slot)
                p, pa = c.parity, PA[(c.parity + k) % 2]
                if k == 6:
                    return
                wait(act, s1_pe, c.n(S1, k + 1))
                if k == 0:
                    cp(xT_hi[:], pa[:, 0:T]).then_inc(s1_act, 1)
                elif k == 1:
                    cp(ks[0:96, p].rearrange("p g t -> p (g t)"), pa[0:96, :]).then_inc(s1_act, 1)
                    cp(vT[96:128].rearrange("p g t -> p (g t)"), pa[96:128, :]).then_inc(s1_act, 1)
                else:
                    j = 2 * (k - 2)
                    cp(qs[0:96, p, j:j + 2].rearrange("p h t -> p (h t)"), pa[0:96, :]).then_inc(s1_act, 1)

            def after(b, slot):
                c = b.shift(-2)
                if c.exists() and slot == 0:
                    wait(act, a_pe, c.n(A_PE, 3))
                    cp(x1T[:], PC[0][:, 0:T]).then_inc(b_act, 1)
                c = b.shift(-1)
                if c.exists() and slot == 0:
                    wait(act, a_dve, c.n(A_DVE, 1))
                    cp(recb[:], recips[:].unsqueeze(3).broadcast_to([P, QT, HEADS, LAT])).then_inc(a_act, 1)
                if c.exists() and slot == 2:
                    wait(act, a_pe, c.n(A_PE, 1))
                    cp(rs_sb[:].rearrange("p g t -> p (g t)"), PC[0][:, :]).then_inc(a_act, 1)
                c = b.shift(-2)
                if c.exists() and slot == 5:
                    wait(act, b_pe, c.n(B_PE, 2))
                    cp(z2T[:], PC[1][:, 0:T]).then_inc(b_act, 1)
                q = b.pair_shift(-2)
                if q.exists() and b.parity == 0 and slot == 2:
                    wait(act, r_dve, q.n(R_DVE, 2))
                    nc.scalar.activation(expd[:], shifted[:], ACT.Exp).then_inc(r_act, 1)

            def step(b):
                for h in range(HEADS):
                    bb, hh = lag(b, h, 1)
                    s1(bb.shift(1), hh)
                    if b.exists():
                        exps(b, h)
                    after(b, h)
                    bb, hh = lag(b, h, 2)
                    if bb.exists():
                        copy_probs(bb, hh)

            pairs_of(act, NB, step, **LAG)

            def step(i):
                c, p = i.shift(1), i.shift(1).parity
                if c.exists():
                    wait(act, t_done, c.n(1, 1))
                    wait(act, up_done, c.n(2, -2))
                    cp(zT[:, p], bank[6 + p][:, 0:BLOCK]).then_inc(zt_done, 1)
                c, p = i, i.parity
                if c.exists():
                    for f in range(FT):
                        if f % 2 == 0:
                            wait(act, up_done, c.n(2, f // 2 + 1))
                        if f == 0:
                            wait(act, down_done, c.n(1, -1))
                        nc.scalar.activation(hT[:, p, f, :],
                                             bank[2 * p + f // 2][:, (f % 2) * BLOCK:(f % 2 + 1) * BLOCK],
                                             ACT.Silu, bias=w1_cur[:, p, F + f:F + f + 1]).then_inc(silu_done, 1)

            pairs_of(act, BLOCKS, step, before=1, after=0)

            def step(i):
                c, p = i, i.parity
                if c.exists():
                    wait(act, fin_pool, c.n(4, 4))
                    wait(act, o_out[p], c.uses() - 16)
                    for t in range(QT):
                        nc.scalar.activation(o_sb[:, p, t], acc[:, p, t], ACT.Identity, bias=nb3[:, p, t:t + 1],
                                             scale=r3[:, p, t:t + 1]).then_inc(fin_act, 1)

            pairs_of(act, NB, step, before=0, after=0)

        @block.vector
        def _(dve):
            v = nc.vector
            links = [0]

            def link(ins):
                links[0] += 1
                ins.then_inc(set_dve, 1)
                dve.wait_ge(set_dve, links[0])

            dve.wait_ge(const_ready, CONSTS)
            dve.wait_ge(set_pe, 3)
            link(v.tensor_copy(vecT[:], bank[3][:, 0:36]))
            link(v.tensor_tensor(mix_sb[:], mix_sb[:], ident[:], ALU.add))
            link(v.tensor_scalar(m1[:], mix_sb[:], vecT[:, 32:33], None, ALU.mult))
            link(v.tensor_scalar(rg[:], rw_sb[:], vecT[:, 34:35], None, ALU.mult))
            link(v.memset(bcol[:], 1.0))
            link(v.tensor_scalar(bcol[:, 0, :], bcol[:, 0, :], vecT[:, 33:34], None, ALU.mult))
            link(v.tensor_scalar(bcol[:, 1, :], bcol[:, 1, :], vecT[:, 35:36], None, ALU.mult))
            link(v.tensor_copy(wkv_hi[:, :, 0:3, :], wkv_sb[:, 0].unsqueeze(2).broadcast_to([P, GROUPS, 3, LAT])))
            v.tensor_copy(wkv_hi[:, :, 3, :], wkv_sb[:, 1])
            link(v.tensor_tensor(wkv_lo[:, :, 0:3, :], wkv_sb[:, 0].unsqueeze(2).broadcast_to([P, GROUPS, 3, LAT]),
                                 wkv_hi[:, :, 0:3, :], ALU.subtract))
            link(v.tensor_tensor(wkv_lo[:, :, 3, :], wkv_sb[:, 1], wkv_hi[:, :, 3, :], ALU.subtract))
            dve.wait_ge(set_pe, 4)
            link(v.tensor_scalar(absq[:].rearrange("p h l -> p (h l)"), bank[4][:, 0:HEADS * LAT], SCALE, None, ALU.mult))
            link(v.tensor_copy(wq_hi[:], absq[:].unsqueeze(2).broadcast_to([P, HEADS, 3, LAT])))
            link(v.tensor_tensor(wq_lo[:], absq[:].unsqueeze(2).broadcast_to([P, HEADS, 3, LAT]), wq_hi[:], ALU.subtract))
            dve.wait_ge(set_pe, 6)
            v.tensor_tensor(c1[:], bank[6][:, 0:P], mixb_bc[:], ALU.add)
            link(v.tensor_copy(rb[:], bank[6][:, P:P + EXPERTS]))
            dve.wait_ge(set_pe, 7)
            v.tensor_tensor(w1_sb[:, :, F:F + FT], bank[7][:, 0:32].rearrange("p (e f) -> p e f", f=FT),
                            vecT[:, 0:32].rearrange("p (e f) -> p e f", f=FT), ALU.add)
            link(v.tensor_scalar(w1_sb[:, :, 0:F], w1_sb[:, :, 0:F], vecT[:, 34:35], None, ALU.mult))
            link(v.memset(keep[:, :, 0:1], 0.0))
            link(v.tensor_copy(base[:], region[:]))
            assert links[0] == SET_DVE, links[0]

            def maxes(b, h):
                p, bk = b.parity, SC[h % 2]
                wait(dve, sc_done, b.n(HB, h + 1))
                for t in range(QT):
                    ins = v.tensor_reduce(negm[:, p, t, h:h + 1], bk[:, t * T:t * T + (t + 1) * P], axis=AX.X,
                                          op=ALU.max, negate=True)
                ins.then_inc(max_done, 1)

            def copy_probs(b, h):
                if h not in ACT_HEADS:
                    wait(dve, pt_done, b.n(HB, h + 1))
                    wait(dve, pv_done, b.n(HB, h - 3))
                    v.tensor_copy(probsT[:, h % 4, :], PT[:, 0:3 * P]).then_inc(pt_dve, 1)

            def s1(c, slot):
                if not c.exists() or slot not in PROJECT_SLOTS:
                    return
                k = PROJECT_SLOTS.index(slot)
                p, pa = c.parity, PA[(c.parity + k) % 2]
                if k == 0:
                    wait(dve, s1_act, c.n(S1, 1))
                    ins = v.tensor_tensor(xT_lo[:], pa[:, 0:T], xT_hi[:], ALU.subtract)
                elif k == 1:
                    wait(dve, s1_act, c.n(S1, 3))
                    low = ks[64:96, p].rearrange("p g t -> p (g t)")
                    ins = v.tensor_tensor(low, pa[64:96, :], low, ALU.subtract)
                elif k == 6:
                    wait(dve, s1_pe, c.n(S1, 7))
                    ins = v.tensor_copy(v_sb[:, p].rearrange("p t g l -> p (t g l)"), pa[:, 0:QT * GROUPS * LAT])
                else:
                    wait(dve, s1_act, c.n(S1, k + 2))
                    j = 2 * (k - 2)
                    low = qs[32:64, p, j:j + 2].rearrange("p h t -> p (h t)")
                    ins = v.tensor_tensor(low, pa[32:64, :], low, ALU.subtract)
                ins.then_inc(s1_dve, 1)

            def latents(b, slot):
                c = b.shift(-1)
                if c.exists() and slot == 3:
                    wait(dve, a_act, c.n(A_ACT, 2))
                    wait(dve, pv_done, c.n(HB, HEADS))
                    v.tensor_tensor(ylT[:].rearrange("p g t -> p (g t)"), YL[:, :],
                                    rs_sb[:].rearrange("p g t -> p (g t)"), ALU.mult).then_inc(a_dve, 1)

            def stats(src, st, mv, done, value):
                wait(dve, done, value(0))
                for t in range(QT):
                    v.bn_stats(st[:, t], src[:, t]).then_inc(done, 1)
                wait_apart(dve, done, value(2), S["apart_dve"])
                for t in range(QT):
                    v.bn_aggr(mv[:, t], st[:, t]).then_inc(done, 1)

            def after(b, slot):
                c = b.shift(-1)
                if c.exists() and slot == 0:
                    wait(dve, exp_done, c.n(HB, HEADS))
                    v.reciprocal(recips[:], sums[:, c.parity]).then_inc(a_dve, 1)
                if c.exists() and slot == 5:
                    wait(dve, a_pe, c.n(A_PE, 2))
                    wait(dve, xr_in[c.parity], c.uses())
                    v.tensor_tensor(a_sb[:], PC[0][:, 0:T].rearrange("p (t d) -> p t d", t=QT), xr[:, c.parity],
                                    ALU.add).then_inc(a_dve, 1)
                    stats(a_sb, st1, mv1, a_dve, lambda k: c.n(A_DVE, 3 + k))
                c = b.shift(-2)
                if c.exists() and slot == 2:
                    wait(dve, b_pe, c.n(B_PE, 1))
                    wait(dve, a_pool, c.n(A_POOL, 9))
                    wait(dve, b_pool, c.n(B_POOL))
                    for t in range(QT):
                        v.scalar_tensor_tensor(x2[:, t], PC[1][:, t * P:(t + 1) * P], rr1[:, t:t + 1], x1c[:, t],
                                               ALU.mult, ALU.add).then_inc(b_dve, 1)
                    stats(x2, st2, mv2, b_dve, lambda k: c.n(B_DVE, 2 + k))
                if c.exists() and slot == 3:
                    wait(dve, b_pool, c.n(B_POOL, 2))
                    for t in range(QT):
                        v.tensor_scalar(z2[:, t], x2[:, t], mv2[:, t, 0:1], r2[:, t:t + 1],
                                        ALU.subtract, ALU.mult).then_inc(b_dve, 1)
                if c.exists() and slot == 7:
                    wait(dve, b_pe, c.n(B_PE, 3))
                    v.tensor_tensor(logits[:, c.parity],
                                    PC[1][:, 0:QT * EXPERTS].rearrange("p (t e) -> p t e", t=QT),
                                    rb[:].unsqueeze(1).broadcast_to([P, QT, EXPERTS]), ALU.add).then_inc(b_dve, 1)

            down8 = iota_down[:].unsqueeze(1).broadcast_to(small)

            def over(t):
                return t.unsqueeze(2).broadcast_to(small)

            def by_expert(t):
                return t.rearrange("p t e -> p e t")

            pair_logits = logits[:].rearrange("p b t e -> p (b t) e")
            ROUTE = [
                lambda q: v.tensor_reduce(top_max[:], pair_logits, axis=AX.X, op=ALU.max),
                lambda q: v.tensor_tensor(shifted[:], pair_logits, over(top_max[:]), ALU.subtract),
                lambda q: v.tensor_reduce(top_sum[:], expd[:], axis=AX.X, op=ALU.add),
                lambda q: v.reciprocal(top_rec[:], top_sum[:]),
                lambda q: v.tensor_tensor(gate[:], expd[:], over(top_rec[:]), ALU.mult),
                lambda q: v.tensor_reduce(top_w[:, 0], gate[:], axis=AX.X, op=ALU.max),
                lambda q: v.tensor_tensor(equal[:], gate[:], over(top_w[:, 0]), ALU.is_equal),
                lambda q: v.tensor_tensor(equal[:], equal[:], down8, ALU.mult),
                lambda q: v.tensor_reduce(rank0[:], equal[:], axis=AX.X, op=ALU.max),
                lambda q: v.tensor_tensor(first_hot[:], down8, over(rank0[:]), ALU.is_equal),
                lambda q: v.scalar_tensor_tensor(gate[:], first_hot[:], -2.0, gate[:], ALU.mult, ALU.add),
                lambda q: v.tensor_reduce(top_w[:, 1], gate[:], axis=AX.X, op=ALU.max),
                lambda q: v.tensor_tensor(equal[:], gate[:], over(top_w[:, 1]), ALU.is_equal),
                lambda q: v.tensor_tensor(equal[:], equal[:], down8, ALU.mult),
                lambda q: v.tensor_reduce(rank1[:], equal[:], axis=AX.X, op=ALU.max),
                lambda q: v.tensor_tensor(second_hot[:], down8, over(rank1[:]), ALU.is_equal),
                lambda q: v.tensor_tensor(both_hot[:], first_hot[:], second_hot[:], ALU.add),
                lambda q: v.tensor_copy(ranks[:].rearrange("p n t e -> p (n t e)"), PC[1][:, 0:2 * RT * EXPERTS]),
                lambda q: v.tensor_copy(counts[:], by_expert(ranks[:, 1])),
                lambda q: v.tensor_tensor(counts[:, :, 0], counts[:, :, 0], base[:], ALU.add),
                lambda q: v.tensor_tensor_scan(totals[:].rearrange("p e t -> p (e t)"),
                                               keep[:].rearrange("p e t -> p (e t)"),
                                               counts[:].rearrange("p e t -> p (e t)"), 0.0, ALU.mult, ALU.add),
                lambda q: v.tensor_tensor(place[:], ranks[:, 0], totals[:].rearrange("p e t -> p t e"), ALU.add),
                lambda q: v.tensor_tensor(place[:], place[:], ranks[:, 1], ALU.subtract),
                lambda q: v.tensor_copy(base[:], totals[:, :, RT - 1]),
                lambda q: v.tensor_tensor(picked[:], first_hot[:], place[:], ALU.mult),
                lambda q: v.tensor_reduce(slots[:, 0], picked[:], axis=AX.X, op=ALU.add),
                lambda q: v.tensor_tensor(picked[:], second_hot[:], place[:], ALU.mult),
                lambda q: v.tensor_reduce(slots[:, 1], picked[:], axis=AX.X, op=ALU.add),
                lambda q: v.tensor_scalar(first_expert[:], rank0[:], -1.0, float(EXPERTS), ALU.mult, ALU.add),
                lambda q: v.tensor_copy(weights[:, :, bass.ds(q.n(RT), RT)], top_w[:]),
            ]
            assert len(ROUTE) == R_DVE
            BY_SLOT = (1, 2, 2, 3, 4, 6, 8, 10, 12, 14, 17, 19, 21, 24, 27, 30)

            def route(b, slot):
                q = b.pair_shift(-2)
                if not q.exists():
                    return
                at = b.parity * HEADS + slot
                for k in range(BY_SLOT[at - 1] if at else 0, BY_SLOT[at]):
                    wait(dve, r_dve, q.n(R_DVE, k))
                    if k == 0:
                        wait(dve, b_dve, b.shift(-4 - b.parity).shift(1).n(B_DVE, B_DVE))
                    if k == 2:
                        wait(dve, r_act, q.n(1, 1))
                    if k == 17:
                        wait(dve, r_pe, q.n(1, 1))
                    if k == 25:
                        wait(dve, queued, q.n(16 * 2 * RT))
                    with nc.allow_low_precision(reason="rows of the queues are whole numbers below 2 ** 24"):
                        ROUTE[k](q).then_inc(r_dve, 1)

            def step(b):
                for h in range(HEADS):
                    latents(b, h)
                    if b.exists():
                        maxes(b, h)
                    bb, hh = lag(b, h, 1)
                    s1(bb.shift(1), hh)
                    bb, hh = lag(b, h, 2)
                    if bb.exists():
                        copy_probs(bb, hh)
                    after(b, h)
                    route(b, h)

            pairs_of(dve, NB, step, **LAG)

            planned = [0]

            def plan(ins):
                planned[0] += 1
                ins.then_inc(plan_dve, 1)
                dve.wait_ge(plan_dve, planned[0])

            dve.wait_ge(r_dve, R_DVE * NB // 2)
            plan(v.tensor_copy(pads_i[:], base[0:1, :]))
            plan(v.scalar_tensor_tensor(amount[:], region[:], -1.0, base[:], ALU.mult, ALU.add))
            many = [P, EXPERTS, TOKENS // BLOCK]
            plan(v.tensor_tensor(filled[:], amount[:].unsqueeze(2).broadcast_to(many),
                                 steps_of[:].unsqueeze(1).broadcast_to(many), ALU.is_gt))
            plan(v.tensor_reduce(n_blocks[:], filled[:], axis=AX.X, op=ALU.add))
            plan(v.tensor_tensor_scan(ends[:], ones8[:], n_blocks[:], 0.0, ALU.mult, ALU.add))
            many = [P, BLOCKS, EXPERTS]
            plan(v.tensor_tensor(past[:], block_no[:].unsqueeze(2).broadcast_to(many),
                                 ends[:].unsqueeze(1).broadcast_to(many), ALU.is_ge))
            plan(v.tensor_tensor(past_n[:], past[:], n_blocks[:].unsqueeze(1).broadcast_to(many), ALU.mult))
            plan(v.tensor_reduce(block_expert[:], past[:], axis=AX.X, op=ALU.add))
            plan(v.tensor_reduce(block_start[:], past_n[:], axis=AX.X, op=ALU.add))
            plan(v.tensor_tensor(block_row[:], block_no[:], block_start[:], ALU.subtract))
            plan(v.tensor_scalar(block_row[:], block_row[:], float(BLOCK), None, ALU.mult))
            plan(v.scalar_tensor_tensor(block_row[:], block_expert[:], float(REGION), block_row[:], ALU.mult, ALU.add))
            plan(v.tensor_copy(rows_i[:], block_row[0:1, :]))
            plan(v.tensor_scalar(block_expert[:], block_expert[:], float(EXPERTS - 1), None, ALU.min))
            plan(v.tensor_copy(experts_i[:], block_expert[0:1, :]))
            assert planned[0] == PLAN
            dve.wait_ge(w_in[4], 32)

            def expert_of(c):
                return dve.value_load(experts_i[0:1, bass.ds(c.n(1), 1)], min_val=0, max_val=EXPERTS - 1)

            def step(i):
                c, p = i.shift(1), i.shift(1).parity
                if c.exists():
                    wait(dve, up_done, c.n(2, -2))
                    wait(dve, silu_done, c.n(FT, -FT))
                    v.tensor_copy(w1_cur[:, p], w1_sb[:, bass.ds(expert_of(c), 1), :].rearrange("p e f -> p (e f)")
                                  ).then_inc(w1_moved, 1)
                c, p = i, i.parity
                if c.exists():
                    wait(dve, xb_in[p], c.uses())
                    wait(dve, dest_done, c.n(2))
                    v.tensor_scalar(other[:], xb[:, p, :, D + 1], block_expert[:, bass.ds(c.n(1), 1)], float(TOKENS),
                                    ALU.not_equal, ALU.mult).then_inc(dest_done, 1)
                    wait(dve, dest_done, c.n(2, 1))
                    wait(dve, y_sent[p], c.uses(32) - 32)
                    v.tensor_tensor(dest[:, p], other[:], xb[:, p, :, D], ALU.add).then_inc(dest_done, 1)
                c, p = i.shift(-1), i.shift(-1).parity
                if c.exists():
                    wait(dve, down_done, c.n(1, 1))
                    wait(dve, y_sent[p], c.uses(32) - 32)
                    v.tensor_tensor(yb[:, p].rearrange("p m d -> p (m d)").rearrange("p (m d) -> p m d", m=2),
                                    bank[4 + p][:, 0:2 * D].rearrange("p (m d) -> p m d", m=2),
                                    b2_bc[:, bass.ds(expert_of(c), 1), :].broadcast_to([P, 2, D]),
                                    ALU.add).then_inc(y_read, 1)

            pairs_of(dve, BLOCKS, step, before=1, after=1)

            def step(i):
                c, p = i, i.parity
                if not c.exists():
                    return
                wait(dve, yv_in[p], c.uses(32))
                wait(dve, fin_act, c.n(2, -2))
                for t in range(QT):
                    tile = bass.ds(c.n(QT, t), 1)
                    v.scalar_tensor_tensor(acc1[:, t], yv[:, p, 0, t], weights[:, 0, tile],
                                           x12[:, tile, :].rearrange("p a d -> p (a d)"),
                                           ALU.mult, ALU.add).then_inc(fin_dve, 1)
                wait(dve, fin_dve, c.n(8, 2))
                for t in range(QT):
                    tile = bass.ds(c.n(QT, t), 1)
                    v.scalar_tensor_tensor(acc[:, p, t], yv[:, p, 1, t], weights[:, 1, tile], acc1[:, t],
                                           ALU.mult, ALU.add).then_inc(fin_dve, 1)
                stats(acc[:, p], st3, mv3[:, p], fin_dve, lambda k: c.n(8, 4 + k))

            pairs_of(dve, NB, step, before=0, after=0)


_INS = ['L0_attn_x', 'L0_attn_wq', 'L0_attn_wk_down', 'L0_attn_wv_down', 'L0_attn_wk_up', 'L0_attn_wv_up', 'L0_attn_wo',
        'L0_ffn_g1', 'L0_ffn_be1', 'L0_ffn_mix_w', 'L0_ffn_mix_b', 'L0_ffn_g2', 'L0_ffn_be2', 'L0_ffn_router_w',
        'L0_ffn_w1', 'L0_ffn_b1', 'L0_ffn_w2', 'L0_ffn_b2']


def kernel(**inputs):
    import numpy as np
    import concourse.bacc as bacc
    from concourse.bass_utils import run_bass_kernel_spmd

    nc = bacc.Bacc("TRN2", target_bir_lowering=False, num_devices=1)
    arrays, args = {}, []
    for name in _INS:
        a = np.ascontiguousarray(inputs[name])
        arrays[f"in_{name}"] = a
        args.append(nc.dram_tensor(f"in_{name}", a.shape, mybir.dt.from_np(a.dtype), kind="ExternalInput").ap())
    shape = inputs["L0_attn_x"].shape
    args.append(nc.dram_tensor("out_0", shape, F32, kind="ExternalOutput").ap())
    build(nc, *args)
    r = run_bass_kernel_spmd(nc, [arrays], core_ids=[0])
    return r.results[0]["out_0"]
```

```python
from contextlib import ExitStack

import concourse.bass as bass
from concourse import mybir

F32 = mybir.dt.float32
I32 = mybir.dt.int32
U32 = mybir.dt.uint32
F32R = mybir.dt.float32r
BF16 = mybir.dt.bfloat16
ALU = mybir.AluOpType
ACT = mybir.ActivationFunctionType
AX = mybir.AxisListType

P = 128
EPS = 1e-5
MASKED = -1e30
NOWHERE = 1e6
HEADS = 8
GROUPS = 2
REP = HEADS // GROUPS
LAT = 32
EXPERTS = 8
BLOCK = 2 * P
ROW = 132
ACT_HEADS = (0, 1, 2, 4, 5, 6)
PROJECT_SLOTS = (0, 2, 3, 4, 5, 6, 7)


class Item:

    def __init__(self, group, off, count, size=4):
        self.group, self.off, self.count, self.size = group, off, count, size
        self.parity, self.slot = off % 2, off % 4

    def shift(self, d):
        return Item(self.group, self.off + d, self.count, self.size)

    def pair_shift(self, d):
        return Item(self.group, self.off // 2 + d, self.count // 2, self.size // 2)

    def exists(self):
        return not isinstance(self.group, int) or 0 <= self.size * self.group + self.off < self.count

    def n(self, per, k=0):
        return self.group * (self.size * per) + (self.off * per + k) if per else k

    def uses(self, per=16, ring=2):
        return self.group * (self.size // ring * per) + (self.off // ring + 1) * per


def wait(eng, sem, value):
    if not isinstance(value, int) or value > 0:
        eng.wait_ge(sem, value)


def wait_apart(eng, sem, value, apart):
    if not isinstance(value, int) or value > 0:
        eng.wait_ge(sem, value)
        eng.sem_inc(apart)


def in_fours(eng, count, step, before=1, after=1, first=1):
    for i in range(-before, 4 * first):
        step(Item(0, i, count))
    if first < count // 4 - 1:
        with eng.Fori(first, count // 4 - 1) as j:
            for off in range(4):
                step(Item(j, off, count))
    for i in range(count - 4, count + after):
        step(Item(0, i, count))


def build(nc, x, wq, wk_down, wv_down, wk_up, wv_up, wo, g1, be1, mix_w, mix_b, g2, be2, router_w, w1, b1, w2, b2, out):
    NB, T, D = x.shape
    F = w1.shape[2]
    FT = F // P
    QT = T // P
    assert D == P and QT == 2 and NB % 8 == 0 and FT == 4
    TILES = NB * QT
    SCALE = float(P) ** -0.5
    HB = HEADS

    x_t = x.rearrange("b (t p) d -> b p t d", p=P)
    pair_t = out.rearrange("b t d -> (b t) d").rearrange("(n t p) d -> n p t d", n=NB // 2, p=P)
    TOKENS = NB * T
    REGION = TOKENS + BLOCK
    BLOCKS = 2 * TOKENS // BLOCK + EXPERTS
    SPARE = EXPERTS * REGION
    assert BLOCKS % 4 == 0
    queue_d = nc.dram_tensor("queue_scratch", [SPARE + EXPERTS * BLOCK, ROW], F32).ap()
    y_d = nc.dram_tensor("y_scratch", [2 * TOKENS, D], F32).ap()
    y_t = y_d.rearrange("(k n t p) d -> n p k t d", k=2, n=NB // 2, p=P)

    with ExitStack() as ctx:
        stay, attention, setup = ctx.enter_context(ExitStack()), ExitStack(), ExitStack()

        def sb(name, shape, dt=F32, part=None):
            return (part or stay).enter_context(nc.sbuf_tensor(name, shape, dt))

        def sem(name):
            return ctx.enter_context(nc.semaphore(name))

        bank = [ctx.enter_context(nc.psum_tensor(f"bank{i}", [P, 512], F32)) for i in range(8)]
        SC, PT, YL, PA, PC = bank[0:2], bank[2], bank[3], bank[4:6], bank[6:8]

        ident = sb("ident", [P, P])
        ident_bf = sb("ident_bf", [P, P], BF16)
        mask_bf = sb("mask_bf", [P, P], BF16)
        half_neg = sb("half_neg", [P, 2 * QT])
        iota_down = sb("iota_down", [P, EXPERTS])
        wkv_sb = sb("wkv_sb", [P, 2, GROUPS, LAT])
        up_sb = sb("up_sb", [LAT, 2, P])
        vec_sb = sb("vec_sb", [36, P])
        upT = sb("upT", [P, 2, LAT])
        wq_hi = sb("wq_hi", [P, HEADS, 3, LAT], F32R)
        wq_lo = sb("wq_lo", [P, HEADS, 3, LAT], F32R)
        wkv_hi = sb("wkv_hi", [P, GROUPS, 4, LAT], F32R)
        wkv_lo = sb("wkv_lo", [P, GROUPS, 4, LAT], F32R)
        wvo = sb("wvo", [P, GROUPS, P])
        vecT = sb("vecT", [P, 36])
        mix_sb = sb("mix_sb", [P, P])
        mixb_bc = sb("mixb_bc", [P, P])
        m1 = sb("m1", [P, P])
        c1 = sb("c1", [P, P])
        rw_sb = sb("rw_sb", [P, EXPERTS])
        rg = sb("rg", [P, EXPERTS])
        rb = sb("rb", [P, EXPERTS])
        bcol = sb("bcol", [P, 2, P])
        w1_sb = sb("w1_sb", [P, EXPERTS, F])
        w1_hi = sb("w1_hi", [P, EXPERTS, F], F32R)
        b1_sb = sb("b1_sb", [P, EXPERTS, FT])
        w2_sb = sb("w2_sb", [P, EXPERTS, FT, D])
        b2_bc = sb("b2_bc", [P, EXPERTS, D])
        earlier = sb("earlier", [P, P], BF16)
        ones_bf = sb("ones_bf", [P, P], BF16)
        pad_rows = sb("pad_rows", [P, 2, ROW])

        x12 = sb("x12", [P, TILES, D])
        rows_i = sb("rows_i", [1, BLOCKS], I32)
        experts_i = sb("experts_i", [1, BLOCKS], I32)

        absq = sb("absq", [P, HEADS, LAT])
        wq_sb = sb("wq_sb", [P, HEADS, P], part=setup)
        wo_sb = sb("wo_sb", [P, HEADS, P], part=setup)
        wqT = sb("wqT", [P, HEADS, P], part=setup)
        setup.close()

        probs = sb("probs", [P, 4, 3 * P], part=attention)
        probsT = sb("probsT", [P, 4, 3 * P], part=attention)
        xq = sb("xq", [P, 2, QT, D], part=attention)
        xr = sb("xr", [P, 2, QT, D], part=attention)
        xT_hi = sb("xT_hi", [P, T], F32R, part=attention)
        xT_lo = sb("xT_lo", [P, T], F32R, part=attention)
        qs = sb("qs", [P, 2, HEADS, T], F32R, part=attention)
        ks = sb("ks", [P, 2, GROUPS, T], F32R, part=attention)
        vT = sb("vT", [P, GROUPS, T], part=attention)
        v_sb = sb("v_sb", [P, 2, QT, GROUPS, LAT], part=attention)
        negm = sb("negm", [P, 2, QT, HEADS], part=attention)
        sums = sb("sums", [P, 2, QT, HEADS], part=attention)
        recips = sb("recips", [P, QT, HEADS], part=attention)
        recb = sb("recb", [P, QT, HEADS, LAT], part=attention)
        rs_sb = sb("rs_sb", [P, GROUPS, T], part=attention)
        ylT = sb("ylT", [P, GROUPS, T], part=attention)

        a_sb = sb("a_sb", [P, QT, D], part=attention)
        st1 = sb("st1", [P, QT, 6], part=attention)
        mv1 = sb("mv1", [P, QT, 2], part=attention)
        ve1 = sb("ve1", [P, QT], part=attention)
        r1 = sb("r1", [P, QT], part=attention)
        u1 = sb("u1", [P, 3, QT], part=attention)
        rr1 = sb("rr1", [P, QT], part=attention)
        x1 = sb("x1", [P, QT, D], part=attention)
        x1c = sb("x1c", [P, QT, D], part=attention)
        x1T = sb("x1T", [P, T], part=attention)
        x2 = sb("x2", [P, QT, D], part=attention)
        st2 = sb("st2", [P, QT, 6], part=attention)
        mv2 = sb("mv2", [P, QT, 2], part=attention)
        ve2 = sb("ve2", [P, QT], part=attention)
        r2 = sb("r2", [P, QT], part=attention)
        rows_all = sb("rows_all", [P, TILES, ROW], part=attention)
        z2 = sb("z2", [P, QT, D], part=attention)
        z2T = sb("z2T", [P, T], part=attention)
        logits = sb("logits", [P, 2, QT, EXPERTS], part=attention)

        RT = 2 * QT
        small = [P, RT, EXPERTS]
        shifted = sb("shifted", small, part=attention)
        expd = sb("expd", small, part=attention)
        gate = sb("gate", small, part=attention)
        equal = sb("equal", small, part=attention)
        first_hot = sb("first_hot", small, part=attention)
        second_hot = sb("second_hot", small, part=attention)
        both_hot = sb("both_hot", small, BF16, part=attention)
        top_max = sb("top_max", [P, RT], part=attention)
        top_sum = sb("top_sum", [P, RT], part=attention)
        top_rec = sb("top_rec", [P, RT], part=attention)
        top_w = sb("top_w", [P, 2, RT], part=attention)
        rank0 = sb("rank0", [P, RT], part=attention)
        rank1 = sb("rank1", [P, RT], part=attention)
        ranks = sb("ranks", [P, 2, RT, EXPERTS], part=attention)
        counts = sb("counts", [P, EXPERTS, RT], part=attention)
        totals = sb("totals", [P, EXPERTS, RT], part=attention)
        keep = sb("keep", [P, EXPERTS, RT], part=attention)
        base = sb("base", [P, EXPERTS], part=attention)
        place = sb("place", small, part=attention)
        picked = sb("picked", small, part=attention)
        slots = sb("slots", [P, 2, 2, RT], U32, part=attention)
        stage = sb("stage", [P, 2, RT, ROW], part=attention)

        steps_of = sb("steps_of", [P, TOKENS // BLOCK], part=attention)
        block_no = sb("block_no", [P, BLOCKS], part=attention)
        region = sb("region", [P, EXPERTS], part=attention)
        amount = sb("amount", [P, EXPERTS], part=attention)
        filled = sb("filled", [P, EXPERTS, TOKENS // BLOCK], part=attention)
        n_blocks = sb("n_blocks", [P, EXPERTS], part=attention)
        ones8 = sb("ones8", [P, EXPERTS], part=attention)
        ends = sb("ends", [P, EXPERTS], part=attention)
        past = sb("past", [P, BLOCKS, EXPERTS], part=attention)
        past_n = sb("past_n", [P, BLOCKS, EXPERTS], part=attention)
        block_expert = sb("block_expert", [P, BLOCKS], part=attention)
        block_start = sb("block_start", [P, BLOCKS], part=attention)
        block_row = sb("block_row", [P, BLOCKS], part=attention)
        pads_i = sb("pads_i", [1, EXPERTS], I32, part=attention)

        attention.close()
        xb = sb("xb", [P, 4, 2, ROW])
        zT_hi = sb("zT_hi", [P, 2, BLOCK], F32R)
        w1_cur = sb("w1_cur", [P, 2, 2, F], F32R)
        b1_cur = sb("b1_cur", [P, 2, FT])
        zT_lo = sb("zT_lo", [P, 2, BLOCK], F32R)
        hT = sb("hT", [P, 2, FT, BLOCK])
        other = sb("other", [P, 2])
        gate_if = sb("gate_if", [P, 2, 2])
        gate_b = sb("gate_b", [P, 2, 2])
        dest = sb("dest", [P, 4, 2], U32)
        yb = sb("yb", [P, 4, 2, D])
        yv = sb("yv", [P, 2, 2, RT, D])
        acc1 = sb("acc1", [P, RT, D])
        acc = sb("acc", [P, 2, RT, D])
        st3 = sb("st3", [P, RT, 6])
        mv3 = sb("mv3", [P, 2, RT, 2])
        ve3 = sb("ve3", [P, RT])
        r3 = sb("r3", [P, 2, RT])
        mr3 = sb("mr3", [P, RT])
        nb3 = sb("nb3", [P, 2, RT])
        o_sb = sb("o_sb", [P, 2, RT, D])

        names = ("w_in0 w_in1 w_in2 w_in3 w_in4 const_ready set_pe set_act set_dve xq_in0 xq_in1 xr_in0 xr_in1 "
                 "s1_pe s1_act s1_dve sc_done max_done exp_done pt_done pt_act pt_dve pv_done "
                 "a_pe a_act a_dve a_pool b_pe b_act b_dve b_pool r_pe r_act r_dve r_pool queued0 queued1 pads_sent "
                 "plan_dve fold_pe fold_act fold_dve apart_pool apart_pe apart_dve apart_sp "
                 "xb_in0 xb_in1 xb_in2 xb_in3 t_done zt_done zt_lo_done w1_hi_moved up_done silu_done "
                 "down_done y_read y_scaled dest_done y_sent0 y_sent1 y_sent2 y_sent3 "
                 "yv_in0 yv_in1 fin_dve fin_pool fin_act o_out0 o_out1").split()
        S = {n: sem(n) for n in names}
        xq_in = [S["xq_in0"], S["xq_in1"]]
        xr_in = [S["xr_in0"], S["xr_in1"]]
        xb_in = [S[f"xb_in{i}"] for i in range(4)]
        y_sent = [S[f"y_sent{i}"] for i in range(4)]
        yv_in = [S["yv_in0"], S["yv_in1"]]
        o_out = [S["o_out0"], S["o_out1"]]
        w_in = [S[f"w_in{i}"] for i in range(5)]
        const_ready, set_pe, set_act, set_dve = (S[n] for n in "const_ready set_pe set_act set_dve".split())
        s1_pe, s1_act, s1_dve = S["s1_pe"], S["s1_act"], S["s1_dve"]
        sc_done, max_done, exp_done, pt_done, pv_done = (S[n] for n in "sc_done max_done exp_done pt_done pv_done".split())
        pt_act, pt_dve = S["pt_act"], S["pt_dve"]
        a_pe, a_act, a_dve, a_pool = (S[n] for n in "a_pe a_act a_dve a_pool".split())
        b_pe, b_act, b_dve, b_pool = (S[n] for n in "b_pe b_act b_dve b_pool".split())
        r_pe, r_act, r_dve, r_pool = (S[n] for n in "r_pe r_act r_dve r_pool".split())
        queued, pads_sent, plan_dve = [S["queued0"], S["queued1"]], S["pads_sent"], S["plan_dve"]
        t_done, zt_done, up_done = (S[n] for n in "t_done zt_done up_done".split())
        silu_done, down_done, y_read, dest_done = (S[n] for n in "silu_done down_done y_read dest_done".split())
        y_scaled, zt_lo_done, w1_hi_moved = S["y_scaled"], S["zt_lo_done"], S["w1_hi_moved"]
        fold_pe, fold_act, fold_dve = S["fold_pe"], S["fold_act"], S["fold_dve"]
        fin_dve, fin_pool, fin_act = (S[n] for n in "fin_dve fin_pool fin_act".split())

        NA = len(ACT_HEADS)
        ND = HEADS - NA
        S1 = 7
        A_PE, A_ACT, A_DVE, A_POOL = 3, 2, 7, 9
        B_PE, B_ACT, B_DVE, B_POOL = 3, 2, 9, 4
        R_DVE = 30
        FIN = 2 + 2 * RT
        QUEUED = 16 * 2 * RT
        PLAN = 15
        SET_DVE = 16
        CONSTS = 19
        LAG = dict(after=6, first=2)

        def copied(eng, b, h):
            if h in ACT_HEADS:
                wait(eng, pt_act, b.n(NA, sum(k <= h for k in ACT_HEADS)))
            else:
                wait(eng, pt_dve, b.n(ND, sum(k <= h and k not in ACT_HEADS for k in range(HEADS))))

        def lag(b, h, d):
            return b.shift((h - d) // HEADS), (h - d) % HEADS

        block = ctx.enter_context(nc.Block())

        @block.sync
        def _(sp):
            sp.dma_start(wq_sb[:], wq.rearrange("d (h k) -> d h k", h=HEADS)).then_inc(w_in[0], 16)
            sp.dma_start(up_sb[:, 0, :], wk_up).then_inc(w_in[0], 16)
            sp.dma_start(up_sb[:, 1, :], wv_up).then_inc(w_in[0], 16)
            sp.dma_start(wkv_sb[:, 0], wk_down.rearrange("d (g l) -> d g l", g=GROUPS)).then_inc(w_in[0], 16)
            sp.dma_start(wkv_sb[:, 1], wv_down.rearrange("d (g l) -> d g l", g=GROUPS)).then_inc(w_in[0], 16)
            sp.dma_start(wo_sb[:], wo.rearrange("(h k) d -> k h d", h=HEADS)).then_inc(w_in[1], 16)
            sp.dma_start(vec_sb[0:32, :], b1.rearrange("e (f p) -> (e f) p", p=P)).then_inc(w_in[2], 16)
            for n, v in enumerate((g1, be1, g2, be2)):
                sp.dma_start(vec_sb[32 + n:33 + n, :], v.rearrange("(a d) -> a d", a=1)).then_inc(w_in[2], 16)
            sp.dma_start(mix_sb[:], mix_w).then_inc(w_in[2], 16)
            sp.dma_start(mixb_bc[:], mix_b.partition_broadcast(P)).then_inc(w_in[2], 16)
            sp.dma_start(rw_sb[:], router_w).then_inc(w_in[2], 16)

            def step(i):
                c, p = i.shift(1), i.shift(1).parity
                if c.exists():
                    wait(sp, s1_pe, c.n(S1, 1 - 2 * S1))
                    sp.dma_start(xq[:, p], x_t[dyn(c)]).then_inc(xq_in[p], 16)
                c, p = i, i.parity
                if c.exists():
                    wait(sp, a_dve, c.n(A_DVE, 3 - 2 * A_DVE))
                    sp.dma_start(xr[:, p], x_t[dyn(c)]).then_inc(xr_in[p], 16)
                if isinstance(i.group, int) and i.off == 2:
                    sp.dma_start(w1_sb[:], w1.rearrange("e d f -> d e f")).then_inc(w_in[3], 16)
                    sp.dma_start(w2_sb[:], w2.rearrange("e (f p) d -> p e f d", p=P)).then_inc(w_in[4], 16)
                    sp.dma_start(b2_bc[:], b2.partition_broadcast(P)).then_inc(w_in[4], 16)

            def dyn(c):
                return c.n(1)

            sp.wait_ge(const_ready, CONSTS)
            for n in range(EXPERTS):
                sp.dma_start(queue_d[SPARE + n * BLOCK:SPARE + (n + 1) * BLOCK, :].rearrange("(m p) d -> p m d", p=P),
                             pad_rows[:]).then_inc(pads_sent, 16)
            in_fours(sp, NB, step, **LAG)
            sp.wait_ge(plan_dve, 1)
            for e in range(EXPERTS):
                end = sp.value_load(pads_i[0:1, e:e + 1], min_val=0, max_val=SPARE - BLOCK)
                sp.dma_start(queue_d[bass.ds(end, BLOCK), :].rearrange("(m p) d -> p m d", p=P),
                             pad_rows[:]).then_inc(pads_sent, 16)
            sp.wait_ge(pads_sent, 2 * EXPERTS * 16)
            for p in range(2):
                sp.wait_ge(queued[p], QUEUED * NB // 4)
            sp.wait_ge(plan_dve, PLAN)

            def step(i):
                c, p = i, i.slot
                if c.exists():
                    row = sp.value_load(rows_i[0:1, bass.ds(c.n(1), 1)], min_val=0, max_val=SPARE + (EXPERTS - 1) * BLOCK)
                    wait_apart(sp, t_done, c.n(1, -3), S["apart_sp"])
                    wait_apart(sp, dest_done, c.n(5, -15), S["apart_sp"])
                    sp.dma_start(xb[:, p], queue_d[bass.ds(row, BLOCK), :].rearrange("(m p) d -> p m d", p=P)
                                 ).then_inc(xb_in[p], 16)

            in_fours(sp, BLOCKS, step, before=0, after=0)
            for p in range(4):
                sp.wait_ge(y_sent[p], 32 * BLOCKS // 4)

            def step(i):
                c, p = i.shift(1), i.shift(1).parity
                if c.exists():
                    wait(sp, fin_dve, c.n(FIN, 2 - 2 * FIN))
                    for k in range(2):
                        sp.dma_start(yv[:, p, k], y_t[c.n(1)][:, k]).then_inc(yv_in[p], 16)
                c, p = i.shift(-1), i.shift(-1).parity
                if c.exists():
                    wait(sp, fin_act, c.n(RT, RT))
                    sp.dma_start(pair_t[c.n(1)], o_sb[:, p]).then_inc(o_out[p], 16)

            in_fours(sp, NB // 2, step, before=2, after=1)
            for p in range(2):
                sp.wait_ge(o_out[p], 16 * NB // 4)

        @block.gpsimd
        def _(pool):
            def const(ins):
                ins.then_inc(const_ready, 1)

            def ramp(t, pattern, start=0, by_row=0):
                const(pool.iota(t, pattern=pattern, base=start, channel_multiplier=by_row,
                                allow_small_or_imprecise_dtypes=True))

            const(pool.memset(ident[:], 0.0))
            const(pool.memset(mask_bf[:], 0.0))
            const(pool.memset(half_neg[:], -0.5))
            ramp(iota_down[:], [[-1, EXPERTS]], start=EXPERTS)
            const(pool.memset(earlier[:], 1.0))
            const(pool.memset(ones_bf[:], 1.0))
            const(pool.memset(pad_rows[:], 0.0))
            const(pool.memset(keep[:], 1.0))
            const(pool.memset(ones8[:], 1.0))
            ramp(region[:], [[REGION, EXPERTS]])
            ramp(steps_of[:], [[BLOCK, TOKENS // BLOCK]])
            ramp(block_no[:], [[1, BLOCKS]])
            const(pool.memset(rows_all[:, :, D:], 0.0))
            pool.wait_ge(const_ready, 13)
            const(pool.affine_select(out=ident[:], in_=ident[:], compare_op=ALU.not_equal, fill=1.0,
                                     base=0, pattern=[[-1, P]], channel_multiplier=1))
            const(pool.affine_select(out=mask_bf[:], in_=mask_bf[:], compare_op=ALU.is_ge, fill=MASKED,
                                     base=0, pattern=[[-1, P]], channel_multiplier=1))
            const(pool.affine_select(out=earlier[:], in_=earlier[:], compare_op=ALU.is_ge, fill=0.0,
                                     base=-1, pattern=[[1, P]], channel_multiplier=-1))
            const(pool.memset(pad_rows[:, :, D:D + 1], NOWHERE))
            ramp(rows_all[:, :, D], [[P, TILES]], by_row=1)
            pool.wait_ge(const_ready, 18)
            pool.tensor_copy(ident_bf[:], ident[:]).then_inc(const_ready, 1)

            def wait(eng, sem, value):
                wait_apart(eng, sem, value, S["apart_pool"])

            def fetch(q):
                if not q.exists():
                    return
                wait(pool, r_dve, q.n(R_DVE, R_DVE))
                wait(pool, b_pool, q.n(2 * B_POOL, 2 * B_POOL))
                if isinstance(q.group, int):
                    pool.sem_inc(r_pool)
                    return
                pool.tensor_copy(stage[:, q.parity], rows_all[:, bass.ds(q.n(RT), RT), :]).then_inc(r_pool, 1)
                wait(pool, r_pool, q.n(1, 1))

            def enqueue(q, which):
                if not q.exists():
                    return
                for n in which:
                    k, t = divmod(n, RT)
                    row = rows_all[:, q.n(RT, t), :] if isinstance(q.group, int) else stage[:, q.parity, t, :]
                    pool.indirect_dma_start(
                        out=queue_d, out_offset=bass.IndirectOffsetOnAxis(ap=slots[:, q.parity, k, t:t + 1], axis=0),
                        in_=row, in_offset=None, bounds_check=SPARE - 1, oob_is_err=False,
                    ).then_inc(queued[q.parity], 16)

            def step(i):
                even = i.parity == 0
                q = i.pair_shift(-3)
                if even:
                    fetch(q)
                c = i.shift(-2)
                if c.exists():
                    wait(pool, b_dve, c.n(B_DVE, 6))
                    pool.tensor_scalar(ve2[:], mv2[:, :, 1], EPS, None, ALU.add, ALU.bypass).then_inc(b_pool, 1)
                    wait(pool, b_pool, c.n(B_POOL, 1))
                    pool.tensor_tensor(r2[:], ve2[:], half_neg[:, 0:QT], ALU.pow).then_inc(b_pool, 1)
                    pool.tensor_tensor(x12[:, bass.ds(c.n(QT), QT), :], x1[:], x2[:], ALU.add).then_inc(b_pool, 1)
                    wait(pool, b_dve, c.n(B_DVE, 8))
                    pool.tensor_copy(rows_all[:, bass.ds(c.n(QT), QT), 0:D], z2[:]).then_inc(b_pool, 1)
                enqueue(q, range(0, 2) if even else range(5, 6))
                c = i.shift(-1)
                if c.exists():
                    wait(pool, a_dve, c.n(A_DVE, 7))
                    pool.tensor_scalar(ve1[:], mv1[:, :, 1], EPS, None, ALU.add, ALU.bypass).then_inc(a_pool, 1)
                    wait(pool, a_pool, c.n(A_POOL, 1))
                    pool.tensor_tensor(r1[:], ve1[:], half_neg[:, 0:QT], ALU.pow).then_inc(a_pool, 1)
                    wait(pool, b_pool, c.n(B_POOL))
                    pool.tensor_tensor(x1[:], a_sb[:], mv1[:, :, 0].unsqueeze(2).broadcast_to([P, QT, D]),
                                       ALU.subtract).then_inc(a_pool, 1)
                    wait(pool, a_pool, c.n(A_POOL, 3))
                    pool.tensor_tensor(x1[:], x1[:], r1[:].unsqueeze(2).broadcast_to([P, QT, D]),
                                       ALU.mult).then_inc(a_pool, 1)
                    wait(pool, a_pool, c.n(A_POOL, 4))
                    pool.tensor_tensor(x1c[:], x1[:], c1[:].unsqueeze(1).broadcast_to([P, QT, D]),
                                       ALU.add).then_inc(a_pool, 1)
                    pool.tensor_tensor(u1[:, 0], mv1[:, :, 1], r1[:], ALU.mult).then_inc(a_pool, 1)
                    wait(pool, a_pool, c.n(A_POOL, 6))
                    pool.tensor_tensor(u1[:, 1], u1[:, 0], r1[:], ALU.mult).then_inc(a_pool, 1)
                    wait(pool, a_pool, c.n(A_POOL, 7))
                    pool.tensor_scalar(u1[:, 2], u1[:, 1], EPS, None, ALU.add, ALU.bypass).then_inc(a_pool, 1)
                    wait(pool, a_pool, c.n(A_POOL, 8))
                    pool.tensor_tensor(rr1[:], u1[:, 2], half_neg[:, 0:QT], ALU.pow).then_inc(a_pool, 1)

                enqueue(q, range(2, 5) if even else range(6, 8))

            in_fours(pool, NB, step, **LAG)

            def step(i):
                c, p = i, i.slot
                if c.exists():
                    wait(pool, y_scaled, c.n(2, 2))
                    wait(pool, dest_done, c.n(5, 5))
                    for m in range(2):
                        pool.indirect_dma_start(
                            out=y_d, out_offset=bass.IndirectOffsetOnAxis(ap=dest[:, p, m:m + 1], axis=0),
                            in_=yb[:, p, m, :], in_offset=None, bounds_check=2 * TOKENS - 1, oob_is_err=False,
                        ).then_inc(y_sent[p], 16)

            in_fours(pool, BLOCKS, step, before=0, after=0)

            def step(i):
                c, p = i, i.parity
                if c.exists():
                    wait(pool, fin_dve, c.n(FIN, FIN))
                    wait(pool, fin_act, c.n(RT, -RT))
                    pool.tensor_scalar(ve3[:], mv3[:, p, :, 1], EPS, None, ALU.add, ALU.bypass).then_inc(fin_pool, 1)
                    wait(pool, fin_pool, c.n(4, 1))
                    pool.tensor_tensor(r3[:, p], ve3[:], half_neg[:], ALU.pow).then_inc(fin_pool, 1)
                    wait(pool, fin_pool, c.n(4, 2))
                    pool.tensor_tensor(mr3[:], mv3[:, p, :, 0], r3[:, p], ALU.mult).then_inc(fin_pool, 1)
                    wait(pool, fin_pool, c.n(4, 3))
                    pool.tensor_scalar(nb3[:, p], mr3[:], -1.0, None, ALU.mult, ALU.bypass).then_inc(fin_pool, 1)

            in_fours(pool, NB // 2, step, before=0, after=0)

        @block.tensor
        def _(pe):
            mm = nc.tensor.matmul
            tr = nc.tensor.transpose

            pe.wait_ge(w_in[0], 80)
            pe.wait_ge(const_ready, CONSTS)
            for n in range(2):
                ins = tr(bank[0][:, n * LAT:(n + 1) * LAT], up_sb[:, n, :], ident[0:LAT, 0:LAT])
            ins.then_inc(set_pe, 1)
            for h in range(HEADS):
                ins = tr(bank[1 + h // 4][:, (h % 4) * P:(h % 4 + 1) * P], wq_sb[:, h, :], ident[:])
            ins.then_inc(set_pe, 1)
            pe.wait_ge(w_in[2], 16 * 8)
            tr(bank[3][:, 0:36], vec_sb[:], ident[0:36, 0:36]).then_inc(set_pe, 1)
            pe.wait_ge(set_act, 2)
            for h in range(HEADS):
                ins = mm(bank[4][:, h * LAT:(h + 1) * LAT], wqT[:, h, :], upT[:, 0, :], start=True, stop=True)
            ins.then_inc(set_pe, 1)
            pe.wait_ge(w_in[1], 16)
            for h in range(HEADS):
                g, r = divmod(h, REP)
                ins = mm(bank[5][LAT * r:LAT * (r + 1), g * P:(g + 1) * P], upT[:, 1, :], wo_sb[:, h, :],
                         start=True, stop=True)
            ins.then_inc(set_pe, 1)
            pe.wait_ge(set_dve, 8)
            mm(bank[6][:, 0:P], bcol[:, 0, :], mix_sb[:], start=True, stop=True)
            mm(bank[6][:, P:P + EXPERTS], bcol[:, 1, :], rw_sb[:], start=True, stop=True).then_inc(set_pe, 1)
            pe.wait_ge(set_act, 3)
            pe.wait_ge(set_dve, SET_DVE)

            def scores(b, h):
                g, p, bk = h // REP, b.parity, SC[h % 2]
                if h == 0:
                    wait(pe, s1_dve, b.n(S1, 2))
                if h % 2 == 0:
                    wait(pe, s1_act, b.n(S1, 4 + h // 2))
                    wait(pe, s1_dve, b.n(S1, 3 + h // 2))
                wait(pe, exp_done, b.n(HB, h - 1))
                for t in range(QT):
                    mm(bk[:, t * T:(t + 1) * T], qs[0:96, p, h, t * P:(t + 1) * P], ks[0:96, p, g, :],
                       start=True, stop=False, skip_group_check=True)
                    ins = mm(bk[:, t * T + t * P:t * T + (t + 1) * P], ident_bf[:], mask_bf[:],
                             start=False, stop=True, skip_group_check=True)
                ins.then_inc(sc_done, 1)

            def transpose_probs(b, h):
                wait(pe, exp_done, b.n(HB, h + 1))
                copied(pe, *lag(b, h, 1))
                for n in range(3):
                    ins = tr(PT[:, n * P:(n + 1) * P], probs[:, h % 4, n * P:(n + 1) * P], ident[:])
                ins.then_inc(pt_done, 1)

            def values(b, h):
                g, r = divmod(h, REP)
                p = b.parity
                copied(pe, b, h)
                if h == 0:
                    wait(pe, s1_dve, b.n(S1, 7))
                    wait(pe, a_dve, b.n(A_DVE, 2 - A_DVE))
                o = YL[LAT * r:LAT * (r + 1), :]
                pt = probsT[:, h % 4, :]
                mm(o[:, g * T:(g + 1) * T], v_sb[:, p, 0, g, :], pt[:, 0:T], start=True, stop=False,
                   skip_group_check=True)
                mm(o[:, g * T + P:(g + 1) * T], v_sb[:, p, 1, g, :], pt[:, T:T + P], start=False, stop=True,
                   skip_group_check=True).then_inc(pv_done, 1)

            def s1(c, slot):
                if not c.exists() or slot not in PROJECT_SLOTS:
                    return
                k = PROJECT_SLOTS.index(slot)
                p, pa = c.parity, PA[(c.parity + k) % 2]
                wait(pe, s1_dve, c.n(S1, k - 1))
                if k == 0:
                    wait(pe, xq_in[p], c.uses())
                    for t in range(QT):
                        ins = tr(pa[:, t * P:(t + 1) * P], xq[:, p, t], ident[:])
                elif k == 6:
                    wait_apart(pe, s1_act, c.n(S1, 3), S["apart_pe"])
                    for t in range(QT):
                        for g in range(GROUPS):
                            o = (t * GROUPS + g) * LAT
                            ins = tr(pa[:, o:o + LAT], vT[96:128, g, t * P:(t + 1) * P], ident[96:128, 96:128])
                else:
                    hi, lo = (wkv_hi, wkv_lo) if k == 1 else (wq_hi, wq_lo)
                    rows = 4 * LAT if k == 1 else 3 * LAT
                    if k == 3:
                        wait(pe, s1_act, c.n(S1, 3))
                    wait(pe, s1_dve, c.n(S1, 1))
                    for n in range(2):
                        j = n if k == 1 else 2 * (k - 2) + n
                        o = pa[0:rows, n * T:(n + 1) * T]
                        w_hi, w_lo = (w[:, j].rearrange("p r l -> p (r l)") for w in (hi, lo))
                        mm(o, w_hi, xT_hi[:], start=True, stop=False)
                        mm(o, w_hi, xT_lo[:], start=False, stop=False)
                        ins = mm(o, w_lo, xT_hi[:], start=False, stop=True)
                ins.then_inc(s1_pe, 1)


            def fold_b1(part):
                if part == 0:
                    pe.wait_ge(w_in[3], 16)
                    pe.wait_ge(s1_act, S1 * NB)
                    pe.wait_ge(s1_dve, S1 * NB)
                for k in range(2 * part, min(2 * part + 2, EXPERTS * FT)):
                    e, f = divmod(k, FT)
                    ins = mm(PA[0][:, k:k + 1], w1_sb[:, e, f * P:(f + 1) * P], vecT[:, 35:36], start=True, stop=True)
                    if k == EXPERTS * FT - 1:
                        ins.then_inc(fold_pe, 1)

            def x1_to_columns(c):
                if c.exists():
                    wait(pe, a_pool, c.n(A_POOL, 4))
                    for t in range(QT):
                        ins = tr(PC[0][:, t * P:(t + 1) * P], x1[:, t], ident[:])
                    ins.then_inc(a_pe, 1)

            def after(b, slot):
                c = b.shift(-1)
                if c.exists() and slot == 1:
                    wait(pe, a_act, c.n(A_ACT, 1))
                    wait(pe, b_act, c.n(B_ACT, 1 - B_ACT))
                    for g in range(GROUPS):
                        for t in range(QT):
                            ins = tr(PC[0][:, (g * QT + t) * P:(g * QT + t + 1) * P],
                                     recb[:, t, g * REP:(g + 1) * REP].rearrange("p h l -> p (h l)"), ident[:])
                    ins.then_inc(a_pe, 1)
                if c.exists() and slot == 4:
                    wait(pe, a_dve, c.n(A_DVE, 2))
                    for t in range(QT):
                        for g in range(GROUPS):
                            ins = mm(PC[0][:, t * P:(t + 1) * P], ylT[:, g, t * P:(t + 1) * P], wvo[:, g, :],
                                     start=g == 0, stop=g == GROUPS - 1)
                    ins.then_inc(a_pe, 1)
                c = b.shift(-2)
                if c.exists() and slot == 1:
                    wait(pe, b_dve, c.n(B_DVE))
                    wait(pe, b_act, c.n(B_ACT, 1))
                    for t in range(QT):
                        ins = mm(PC[1][:, t * P:(t + 1) * P], x1T[:, t * P:(t + 1) * P], m1[:], start=True, stop=True)
                    ins.then_inc(b_pe, 1)
                q = b.pair_shift(-2)
                if q.exists() and b.parity == 1 and slot == 3:
                    wait(pe, r_dve, q.n(R_DVE, 17))
                    wait(pe, b_dve, b.shift(-2).n(B_DVE, 2) if b.shift(-2).exists() else 0)
                    hot = both_hot[:].rearrange("p t e -> p (t e)")
                    n = RT * EXPERTS
                    mm(PC[1][:, 0:n], earlier[:], hot, start=True, stop=True)
                    mm(PC[1][:, n:2 * n], ones_bf[:], hot, start=True, stop=True).then_inc(r_pe, 1)
                if c.exists() and slot == 4:
                    wait(pe, b_dve, c.n(B_DVE, 8))
                    q = b.pair_shift(-2)
                    wait(pe, r_dve, (q.n(R_DVE, 18) if b.parity == 1 else q.n(R_DVE, 18 - R_DVE)) if q.exists() or
                         b.parity == 0 else 0)
                    for t in range(QT):
                        ins = tr(PC[1][:, t * P:(t + 1) * P], z2[:, t], ident[:])
                    ins.then_inc(b_pe, 1)
                if c.exists() and slot == 6:
                    wait(pe, b_act, c.n(B_ACT, 2))
                    for t in range(QT):
                        ins = mm(PC[1][:, t * EXPERTS:(t + 1) * EXPERTS], z2T[:, t * P:(t + 1) * P], rg[:],
                                 start=True, stop=True)
                    ins.then_inc(b_pe, 1)

            def step(b):
                for h in range(HEADS):
                    bb, hh = lag(b, h, -1)
                    if bb.exists():
                        scores(bb, hh)
                    bb, hh = lag(b, h, 4)
                    if bb.exists():
                        values(bb, hh)
                    s1(b.shift(1), h)
                    after(b, h)
                    bb, hh = lag(b, h, 2)
                    if bb.exists():
                        transpose_probs(bb, hh)
                    if h == 7:
                        x1_to_columns(b.shift(-1))
                    if isinstance(b.group, int) and b.off >= NB:
                        fold_b1((b.off - NB) * HEADS + h)

            in_fours(pe, NB, step, **LAG)

            pe.wait_ge(fold_dve, EXPERTS + 1)
            pe.wait_ge(w_in[4], 32)
            pe.wait_ge(plan_dve, PLAN)

            def expert_of(eng, c):
                return eng.value_load(experts_i[0:1, bass.ds(c.n(1), 1)], min_val=0, max_val=EXPERTS - 1)

            def rows_to_columns(c):
                p = c.parity
                wait(pe, xb_in[c.slot], c.uses(ring=4))
                for m in range(2):
                    ins = tr(bank[6 + p][:, m * P:(m + 1) * P], xb[:, c.slot, m, 0:D], ident[:])
                ins.then_inc(t_done, 1)

            def up(c):
                p = c.parity
                wait(pe, w1_hi_moved, c.n(1, 1))
                wait(pe, zt_lo_done, c.n(1, 1))
                for f in range(FT):
                    o = bank[2 * p + f // 2][:, (f % 2) * BLOCK:(f % 2 + 1) * BLOCK]
                    hi, lo = (w1_cur[:, p, n, f * P:(f + 1) * P] for n in range(2))
                    mm(o, hi, zT_hi[:, p], start=True, stop=False)
                    mm(o, hi, zT_lo[:, p], start=False, stop=False)
                    ins = mm(o, lo, zT_hi[:, p], start=False, stop=True)
                    if f % 2:
                        ins.then_inc(up_done, 1)

            def down(c, e):
                p = c.parity
                wait(pe, silu_done, c.n(FT, FT))
                wait(pe, y_read, c.n(1, -1))
                for m in range(2):
                    for f in range(FT):
                        ins = mm(bank[4 + p][:, m * P:(m + 1) * P], hT[:, p, f, m * P:(m + 1) * P],
                                 w2_sb[:, bass.ds(e, 1), f, :].rearrange("p e d -> p (e d)"),
                                 start=f == 0, stop=f == FT - 1)
                ins.then_inc(down_done, 1)

            def step(i):
                before = i.shift(-1)
                e = expert_of(pe, before) if before.exists() else None
                if i.exists():
                    up(i)
                if i.shift(2).exists():
                    rows_to_columns(i.shift(2))
                if before.exists():
                    down(before, e)

            in_fours(pe, BLOCKS, step, before=2, after=1)

        @block.scalar
        def _(act):
            cp = nc.scalar.copy
            act.wait_ge(set_pe, 1)
            cp(upT[:].rearrange("p n l -> p (n l)"), bank[0][:, 0:2 * LAT]).then_inc(set_act, 1)
            act.wait_ge(set_pe, 2)
            cp(wqT[:, 0:4].rearrange("p h k -> p (h k)"), bank[1][:])
            cp(wqT[:, 4:8].rearrange("p h k -> p (h k)"), bank[2][:]).then_inc(set_act, 1)
            act.wait_ge(set_pe, 5)
            cp(wvo[:].rearrange("p g k -> p (g k)"), bank[5][:, 0:2 * P]).then_inc(set_act, 1)
            act.wait_ge(set_dve, SET_DVE)

            def exps(b, h):
                p, bk = b.parity, SC[h % 2]
                wait(act, max_done, b.n(HB, h + 1))
                wait(act, pt_done, b.n(HB, h - 3))
                for t in range(QT):
                    ins = nc.scalar.activation(probs[:, h % 4, t * P:(t + 1 + t) * P], bk[:, t * T:t * T + (t + 1) * P],
                                               ACT.Exp, bias=negm[:, p, t, h:h + 1], accum_out=sums[:, p, t, h:h + 1])
                ins.then_inc(exp_done, 1)

            def copy_probs(b, h):
                if h in ACT_HEADS:
                    wait(act, pt_done, b.n(HB, h + 1))
                    wait(act, pv_done, b.n(HB, h - 3))
                    cp(probsT[:, h % 4, :], PT[:, 0:3 * P]).then_inc(pt_act, 1)

            def s1(c, slot):
                if not c.exists() or slot not in PROJECT_SLOTS:
                    return
                k = PROJECT_SLOTS.index(slot)
                p, pa = c.parity, PA[(c.parity + k) % 2]
                if k == 6:
                    return
                wait(act, s1_pe, c.n(S1, k + 1))
                if k == 0:
                    cp(xT_hi[:], pa[:, 0:T]).then_inc(s1_act, 1)
                elif k == 1:
                    cp(ks[0:96, p].rearrange("p g t -> p (g t)"), pa[0:96, :]).then_inc(s1_act, 1)
                else:
                    j = 2 * (k - 2)
                    cp(qs[0:96, p, j:j + 2].rearrange("p h t -> p (h t)"), pa[0:96, :]).then_inc(s1_act, 1)

            def s1_v(c, slot):
                if c.exists() and slot == PROJECT_SLOTS[1]:
                    pa = PA[(c.parity + 1) % 2]
                    cp(vT[96:128].rearrange("p g t -> p (g t)"), pa[96:128, :]).then_inc(s1_act, 1)

            def after(b, slot):
                c = b.shift(-2)
                if c.exists() and slot == 0:
                    wait(act, a_pe, c.n(A_PE, 3))
                    cp(x1T[:], PC[0][:, 0:T]).then_inc(b_act, 1)
                c = b.shift(-1)
                if c.exists() and slot == 0:
                    wait(act, a_dve, c.n(A_DVE, 1))
                    cp(recb[:], recips[:].unsqueeze(3).broadcast_to([P, QT, HEADS, LAT])).then_inc(a_act, 1)
                if c.exists() and slot == 2:
                    wait(act, a_pe, c.n(A_PE, 1))
                    cp(rs_sb[:].rearrange("p g t -> p (g t)"), PC[0][:, :]).then_inc(a_act, 1)
                c = b.shift(-2)
                if c.exists() and slot == 5:
                    wait(act, b_pe, c.n(B_PE, 2))
                    cp(z2T[:], PC[1][:, 0:T]).then_inc(b_act, 1)
                q = b.pair_shift(-2)
                if q.exists() and b.parity == 0 and slot == 2:
                    wait(act, r_dve, q.n(R_DVE, 2))
                    nc.scalar.activation(expd[:], shifted[:], ACT.Exp).then_inc(r_act, 1)

            def step(b):
                for h in range(HEADS):
                    bb, hh = lag(b, h, 1)
                    s1(bb.shift(1), hh)
                    b3, h3 = lag(b, h, 3)
                    if b3.exists():
                        copy_probs(b3, h3)
                    if b.exists():
                        exps(b, h)
                    s1_v(bb.shift(1), hh)
                    after(b, h)

            in_fours(act, NB, step, **LAG)

            act.wait_ge(w_in[3], 16)
            for e in range(EXPERTS):
                nc.scalar.activation(w1_hi[:, e], w1_sb[:, e], ACT.Copy, scale=vecT[:, 34:35]).then_inc(fold_act, 1)
            act.wait_ge(fold_act, EXPERTS)
            act.wait_ge(fold_dve, EXPERTS + 1)
            act.wait_ge(plan_dve, PLAN)

            def step(i):
                c, p = i, i.parity
                if c.exists():
                    for f in range(FT):
                        if f % 2 == 0:
                            wait(act, up_done, c.n(2, f // 2 + 1))
                        if f == 0:
                            wait(act, down_done, c.n(1, -1))
                        nc.scalar.activation(hT[:, p, f, :],
                                             bank[2 * p + f // 2][:, (f % 2) * BLOCK:(f % 2 + 1) * BLOCK],
                                             ACT.Silu, bias=b1_cur[:, p, f:f + 1]).then_inc(silu_done, 1)
                c, p = i.shift(2), i.shift(2).parity
                if c.exists():
                    e = act.value_load(experts_i[0:1, bass.ds(c.n(1), 1)], min_val=0, max_val=EXPERTS - 1)
                    wait(act, t_done, c.n(1, 1))
                    cp(zT_hi[:, p], bank[6 + p][:, 0:BLOCK]).then_inc(zt_done, 1)
                    cp(w1_cur[:, p, 0], w1_hi[:, bass.ds(e, 1), :].rearrange("p e f -> p (e f)")).then_inc(w1_hi_moved, 1)

            in_fours(act, BLOCKS, step, before=2, after=0)

            def step(i):
                c, p = i, i.parity
                if c.exists():
                    wait(act, fin_pool, c.n(4, 4))
                    wait(act, o_out[p], c.uses() - 16)
                    for t in range(RT):
                        nc.scalar.activation(o_sb[:, p, t], acc[:, p, t], ACT.Identity, bias=nb3[:, p, t:t + 1],
                                             scale=r3[:, p, t:t + 1]).then_inc(fin_act, 1)

            in_fours(act, NB // 2, step, before=0, after=0)

        @block.vector
        def _(dve):
            v = nc.vector
            links = [0]

            def link(ins):
                links[0] += 1
                ins.then_inc(set_dve, 1)
                dve.wait_ge(set_dve, links[0])

            dve.wait_ge(const_ready, CONSTS)
            dve.wait_ge(set_pe, 3)
            link(v.tensor_copy(vecT[:], bank[3][:, 0:36]))
            link(v.tensor_tensor(mix_sb[:], mix_sb[:], ident[:], ALU.add))
            link(v.tensor_scalar(m1[:], mix_sb[:], vecT[:, 32:33], None, ALU.mult))
            link(v.tensor_scalar(rg[:], rw_sb[:], vecT[:, 34:35], None, ALU.mult))
            link(v.memset(bcol[:], 1.0))
            link(v.tensor_scalar(bcol[:, 0, :], bcol[:, 0, :], vecT[:, 33:34], None, ALU.mult))
            link(v.tensor_scalar(bcol[:, 1, :], bcol[:, 1, :], vecT[:, 35:36], None, ALU.mult))
            link(v.tensor_copy(wkv_hi[:, :, 0:3, :], wkv_sb[:, 0].unsqueeze(2).broadcast_to([P, GROUPS, 3, LAT])))
            v.tensor_copy(wkv_hi[:, :, 3, :], wkv_sb[:, 1])
            link(v.tensor_tensor(wkv_lo[:, :, 0:3, :], wkv_sb[:, 0].unsqueeze(2).broadcast_to([P, GROUPS, 3, LAT]),
                                 wkv_hi[:, :, 0:3, :], ALU.subtract))
            link(v.tensor_tensor(wkv_lo[:, :, 3, :], wkv_sb[:, 1], wkv_hi[:, :, 3, :], ALU.subtract))
            dve.wait_ge(set_pe, 4)
            link(v.tensor_scalar(absq[:].rearrange("p h l -> p (h l)"), bank[4][:, 0:HEADS * LAT], SCALE, None, ALU.mult))
            link(v.tensor_copy(wq_hi[:], absq[:].unsqueeze(2).broadcast_to([P, HEADS, 3, LAT])))
            link(v.tensor_tensor(wq_lo[:], absq[:].unsqueeze(2).broadcast_to([P, HEADS, 3, LAT]), wq_hi[:], ALU.subtract))
            dve.wait_ge(set_pe, 6)
            v.tensor_tensor(c1[:], bank[6][:, 0:P], mixb_bc[:], ALU.add)
            link(v.tensor_copy(rb[:], bank[6][:, P:P + EXPERTS]))
            link(v.memset(keep[:, :, 0:1], 0.0))
            link(v.tensor_copy(base[:], region[:]))
            assert links[0] == SET_DVE, links[0]

            def maxes(b, h):
                p, bk = b.parity, SC[h % 2]
                wait(dve, sc_done, b.n(HB, h + 1))
                for t in range(QT):
                    ins = v.tensor_reduce(negm[:, p, t, h:h + 1], bk[:, t * T:t * T + (t + 1) * P], axis=AX.X,
                                          op=ALU.max, negate=True)
                ins.then_inc(max_done, 1)

            def copy_probs(b, h):
                if h not in ACT_HEADS:
                    wait(dve, pt_done, b.n(HB, h + 1))
                    wait(dve, pv_done, b.n(HB, h - 3))
                    v.tensor_copy(probsT[:, h % 4, :], PT[:, 0:3 * P]).then_inc(pt_dve, 1)

            def s1(c, slot):
                if not c.exists() or slot not in PROJECT_SLOTS:
                    return
                k = PROJECT_SLOTS.index(slot)
                p, pa = c.parity, PA[(c.parity + k) % 2]
                if k == 0:
                    wait(dve, s1_act, c.n(S1, 1))
                    ins = v.tensor_tensor(xT_lo[:], pa[:, 0:T], xT_hi[:], ALU.subtract)
                elif k == 1:
                    wait(dve, s1_act, c.n(S1, 2))
                    low = ks[64:96, p].rearrange("p g t -> p (g t)")
                    ins = v.tensor_tensor(low, pa[64:96, :], low, ALU.subtract)
                elif k == 6:
                    wait(dve, s1_pe, c.n(S1, 7))
                    ins = v.tensor_copy(v_sb[:, p].rearrange("p t g l -> p (t g l)"), pa[:, 0:QT * GROUPS * LAT])
                else:
                    wait(dve, s1_act, c.n(S1, k + 2))
                    j = 2 * (k - 2)
                    low = qs[32:64, p, j:j + 2].rearrange("p h t -> p (h t)")
                    ins = v.tensor_tensor(low, pa[32:64, :], low, ALU.subtract)
                ins.then_inc(s1_dve, 1)

            def latents(b, slot):
                c = b.shift(-1)
                if c.exists() and slot == 3:
                    wait(dve, a_act, c.n(A_ACT, 2))
                    wait(dve, pv_done, c.n(HB, HEADS))
                    v.tensor_tensor(ylT[:].rearrange("p g t -> p (g t)"), YL[:, :],
                                    rs_sb[:].rearrange("p g t -> p (g t)"), ALU.mult).then_inc(a_dve, 1)

            def stats(src, st, mv, done, value, between=lambda: None):
                between()
                wait(dve, done, value(0))
                for t in range(QT):
                    v.bn_stats(st[:, t], src[:, t]).then_inc(done, 1)
                between()
                wait_apart(dve, done, value(2), S["apart_dve"])
                for t in range(QT):
                    v.bn_aggr(mv[:, t], st[:, t]).then_inc(done, 1)

            def after(b, slot, between):
                c = b.shift(-1)
                if c.exists() and slot == 0:
                    wait(dve, exp_done, c.n(HB, HEADS))
                    v.reciprocal(recips[:], sums[:, c.parity]).then_inc(a_dve, 1)
                if c.exists() and slot == 5:
                    wait(dve, a_pe, c.n(A_PE, 2))
                    wait(dve, xr_in[c.parity], c.uses())
                    v.tensor_tensor(a_sb[:], PC[0][:, 0:T].rearrange("p (t d) -> p t d", t=QT), xr[:, c.parity],
                                    ALU.add).then_inc(a_dve, 1)
                    stats(a_sb, st1, mv1, a_dve, lambda k: c.n(A_DVE, 3 + k), between)
                c = b.shift(-2)
                if c.exists() and slot == 2:
                    wait(dve, b_pe, c.n(B_PE, 1))
                    wait(dve, a_pool, c.n(A_POOL, 9))
                    wait(dve, b_pool, c.n(B_POOL))
                    for t in range(QT):
                        v.scalar_tensor_tensor(x2[:, t], PC[1][:, t * P:(t + 1) * P], rr1[:, t:t + 1], x1c[:, t],
                                               ALU.mult, ALU.add).then_inc(b_dve, 1)
                    stats(x2, st2, mv2, b_dve, lambda k: c.n(B_DVE, 2 + k), between)
                if c.exists() and slot == 3:
                    wait(dve, b_pool, c.n(B_POOL, 2))
                    for t in range(QT):
                        v.tensor_scalar(z2[:, t], x2[:, t], mv2[:, t, 0:1], r2[:, t:t + 1],
                                        ALU.subtract, ALU.mult).then_inc(b_dve, 1)
                if c.exists() and slot == 7:
                    wait(dve, b_pe, c.n(B_PE, 3))
                    v.tensor_tensor(logits[:, c.parity],
                                    PC[1][:, 0:QT * EXPERTS].rearrange("p (t e) -> p t e", t=QT),
                                    rb[:].unsqueeze(1).broadcast_to([P, QT, EXPERTS]), ALU.add).then_inc(b_dve, 1)

            down8 = iota_down[:].unsqueeze(1).broadcast_to(small)

            def over(t):
                return t.unsqueeze(2).broadcast_to(small)

            def by_expert(t):
                return t.rearrange("p t e -> p e t")

            pair_logits = logits[:].rearrange("p b t e -> p (b t) e")
            ROUTE = [
                lambda q: v.tensor_reduce(top_max[:], pair_logits, axis=AX.X, op=ALU.max),
                lambda q: v.tensor_tensor(shifted[:], pair_logits, over(top_max[:]), ALU.subtract),
                lambda q: v.tensor_reduce(top_sum[:], expd[:], axis=AX.X, op=ALU.add),
                lambda q: v.reciprocal(top_rec[:], top_sum[:]),
                lambda q: v.tensor_tensor(gate[:], expd[:], over(top_rec[:]), ALU.mult),
                lambda q: v.tensor_reduce(top_w[:, 0], gate[:], axis=AX.X, op=ALU.max),
                lambda q: v.tensor_tensor(equal[:], gate[:], over(top_w[:, 0]), ALU.is_equal),
                lambda q: v.tensor_tensor(equal[:], equal[:], down8, ALU.mult),
                lambda q: v.tensor_reduce(rank0[:], equal[:], axis=AX.X, op=ALU.max),
                lambda q: v.tensor_tensor(first_hot[:], down8, over(rank0[:]), ALU.is_equal),
                lambda q: v.scalar_tensor_tensor(gate[:], first_hot[:], -2.0, gate[:], ALU.mult, ALU.add),
                lambda q: v.tensor_reduce(top_w[:, 1], gate[:], axis=AX.X, op=ALU.max),
                lambda q: v.tensor_tensor(equal[:], gate[:], over(top_w[:, 1]), ALU.is_equal),
                lambda q: v.tensor_tensor(equal[:], equal[:], down8, ALU.mult),
                lambda q: v.tensor_reduce(rank1[:], equal[:], axis=AX.X, op=ALU.max),
                lambda q: v.tensor_tensor(second_hot[:], down8, over(rank1[:]), ALU.is_equal),
                lambda q: v.tensor_tensor(both_hot[:], first_hot[:], second_hot[:], ALU.add),
                lambda q: v.tensor_copy(ranks[:].rearrange("p n t e -> p (n t e)"), PC[1][:, 0:2 * RT * EXPERTS]),
                lambda q: v.tensor_copy(counts[:], by_expert(ranks[:, 1])),
                lambda q: v.tensor_tensor(counts[:, :, 0], counts[:, :, 0], base[:], ALU.add),
                lambda q: v.tensor_tensor_scan(totals[:].rearrange("p e t -> p (e t)"),
                                               keep[:].rearrange("p e t -> p (e t)"),
                                               counts[:].rearrange("p e t -> p (e t)"), 0.0, ALU.mult, ALU.add),
                lambda q: v.tensor_tensor(place[:], ranks[:, 0], totals[:].rearrange("p e t -> p t e"), ALU.add),
                lambda q: v.tensor_tensor(place[:], place[:], ranks[:, 1], ALU.subtract),
                lambda q: v.tensor_copy(base[:], totals[:, :, RT - 1]),
                lambda q: v.tensor_tensor(picked[:], first_hot[:], place[:], ALU.mult),
                lambda q: v.tensor_reduce(slots[:, q.parity, 0], picked[:], axis=AX.X, op=ALU.add),
                lambda q: v.tensor_tensor(picked[:], second_hot[:], place[:], ALU.mult),
                lambda q: v.tensor_reduce(slots[:, q.parity, 1], picked[:], axis=AX.X, op=ALU.add),
                lambda q: v.tensor_scalar(rows_all[:, bass.ds(q.n(RT), RT), D + 1], rank0[:], -1.0, float(EXPERTS),
                                          ALU.mult, ALU.add),
                lambda q: v.tensor_copy(rows_all[:, bass.ds(q.n(RT), RT), D + 2:], top_w[:].rearrange("p k t -> p t k")),
            ]
            assert len(ROUTE) == R_DVE
            BY_SLOT = (1, 2, 2, 4, 6, 8, 10, 12, 14, 16, 17, 17, 21, 24, 27, 30)

            def route(b, k):
                q = b.pair_shift(-2)
                if not q.exists():
                    return
                wait(dve, r_dve, q.n(R_DVE, k))
                if k == 0:
                    wait(dve, b_dve, b.shift(-4 - b.parity).shift(1).n(B_DVE, B_DVE))
                if k == 2:
                    wait(dve, r_act, q.n(1, 1))
                if k == 17:
                    wait(dve, r_pe, q.n(1, 1))
                if k == 25:
                    wait(dve, queued[q.parity], q.uses(QUEUED) - QUEUED)
                with nc.allow_low_precision(reason="rows of the queues are whole numbers below 2 ** 24"):
                    ROUTE[k](q).then_inc(r_dve, 1)

            def step(b):
                for h in range(HEADS):
                    at = b.parity * HEADS + h
                    left = list(range(BY_SLOT[at - 1] if at else 0, BY_SLOT[at]))

                    def between():
                        if left:
                            route(b, left.pop(0))

                    latents(b, h)
                    bb, hh = lag(b, h, 3)
                    if bb.exists():
                        copy_probs(bb, hh)
                    if len(left) > 3:
                        between()
                    bb, hh = lag(b, h, 1)
                    s1(bb.shift(1), hh)
                    between()
                    bb, hh = lag(b, h, -1)
                    if bb.exists():
                        maxes(bb, hh)
                    between()
                    after(b, h, between)
                    while left:
                        between()

            in_fours(dve, NB, step, **LAG)

            planned = [0]

            def plan(ins):
                planned[0] += 1
                ins.then_inc(plan_dve, 1)
                dve.wait_ge(plan_dve, planned[0])

            dve.wait_ge(r_dve, R_DVE * NB // 2)
            plan(v.tensor_copy(pads_i[:], base[0:1, :]))
            plan(v.scalar_tensor_tensor(amount[:], region[:], -1.0, base[:], ALU.mult, ALU.add))
            many = [P, EXPERTS, TOKENS // BLOCK]
            plan(v.tensor_tensor(filled[:], amount[:].unsqueeze(2).broadcast_to(many),
                                 steps_of[:].unsqueeze(1).broadcast_to(many), ALU.is_gt))
            plan(v.tensor_reduce(n_blocks[:], filled[:], axis=AX.X, op=ALU.add))
            plan(v.tensor_tensor_scan(ends[:], ones8[:], n_blocks[:], 0.0, ALU.mult, ALU.add))
            many = [P, BLOCKS, EXPERTS]
            plan(v.tensor_tensor(past[:], block_no[:].unsqueeze(2).broadcast_to(many),
                                 ends[:].unsqueeze(1).broadcast_to(many), ALU.is_ge))
            plan(v.tensor_tensor(past_n[:], past[:], n_blocks[:].unsqueeze(1).broadcast_to(many), ALU.mult))
            plan(v.tensor_reduce(block_expert[:], past[:], axis=AX.X, op=ALU.add))
            plan(v.tensor_reduce(block_start[:], past_n[:], axis=AX.X, op=ALU.add))
            plan(v.tensor_tensor(block_row[:], block_no[:], block_start[:], ALU.subtract))
            plan(v.tensor_scalar(block_row[:], block_row[:], float(BLOCK), None, ALU.mult))
            plan(v.scalar_tensor_tensor(block_row[:], block_expert[:], float(REGION), block_row[:], ALU.mult, ALU.add))
            plan(v.tensor_copy(rows_i[:], block_row[0:1, :]))
            plan(v.tensor_scalar(block_expert[:], block_expert[:], float(EXPERTS - 1), None, ALU.min))
            plan(v.tensor_copy(experts_i[:], block_expert[0:1, :]))
            assert planned[0] == PLAN
            dve.wait_ge(fold_pe, 1)
            dve.wait_ge(fold_act, EXPERTS)
            v.tensor_tensor(b1_sb[:], PA[0][:, 0:EXPERTS * FT].rearrange("p (e f) -> p e f", f=FT),
                            vecT[:, 0:32].rearrange("p (e f) -> p e f", f=FT), ALU.add).then_inc(fold_dve, 1)
            for e in range(EXPERTS):
                v.scalar_tensor_tensor(w1_sb[:, e], w1_sb[:, e], vecT[:, 34:35], w1_hi[:, e],
                                       ALU.mult, ALU.subtract).then_inc(fold_dve, 1)
            dve.wait_ge(fold_dve, EXPERTS + 1)
            dve.wait_ge(w_in[4], 32)

            def expert_of(c):
                return dve.value_load(experts_i[0:1, bass.ds(c.n(1), 1)], min_val=0, max_val=EXPERTS - 1)

            def step(i):
                c, p = i, i.slot
                if c.exists():
                    first, expert = xb[:, p, :, D + 1], block_expert[:, bass.ds(c.n(1), 1)]
                    wait(dve, xb_in[p], c.uses(ring=4))
                    wait(dve, dest_done, c.n(5))
                    v.tensor_scalar(other[:], first, expert, float(TOKENS), ALU.not_equal, ALU.mult).then_inc(dest_done, 1)
                    v.scalar_tensor_tensor(gate_if[:, 0], first, expert, xb[:, p, :, D + 2],
                                           ALU.is_equal, ALU.mult).then_inc(dest_done, 1)
                    v.scalar_tensor_tensor(gate_if[:, 1], first, expert, xb[:, p, :, D + 3],
                                           ALU.not_equal, ALU.mult).then_inc(dest_done, 1)
                    wait(dve, dest_done, c.n(5, 3))
                    wait(dve, y_sent[p], c.uses(32, ring=4) - 32)
                    v.tensor_tensor(dest[:, p], other[:], xb[:, p, :, D], ALU.add).then_inc(dest_done, 1)
                    v.tensor_tensor(gate_b[:, c.parity], gate_if[:, 0], gate_if[:, 1], ALU.add).then_inc(dest_done, 1)
                c, p = i.shift(2), i.shift(2).parity
                if c.exists():
                    e = expert_of(c)
                    wait(dve, silu_done, c.n(FT, -FT))
                    v.tensor_copy(w1_cur[:, p, 1], w1_sb[:, bass.ds(e, 1), :].rearrange("p e f -> p (e f)"))
                    v.tensor_copy(b1_cur[:, p], b1_sb[:, bass.ds(e, 1), :].rearrange("p e f -> p (e f)"))
                    wait(dve, zt_done, c.n(1, 1))
                    v.tensor_tensor(zT_lo[:, p], bank[6 + p][:, 0:BLOCK], zT_hi[:, p], ALU.subtract
                                    ).then_inc(zt_lo_done, 1)
                c, p = i.shift(-1), i.shift(-1).parity
                if c.exists():
                    e = expert_of(c)
                    wait(dve, down_done, c.n(1, 1))
                    v.tensor_tensor(yb[:, c.slot],
                                    bank[4 + p][:, 0:2 * D].rearrange("p (m d) -> p m d", m=2),
                                    b2_bc[:, bass.ds(e, 1), :].broadcast_to([P, 2, D]),
                                    ALU.add).then_inc(y_read, 1)
                    wait(dve, y_read, c.n(1, 1))
                    for m in range(2):
                        v.tensor_scalar(yb[:, c.slot, m], yb[:, c.slot, m], gate_b[:, p, m:m + 1], None,
                                        ALU.mult).then_inc(y_scaled, 1)

            in_fours(dve, BLOCKS, step, before=2, after=1)

            def step(i):
                c, p = i, i.parity
                if not c.exists():
                    return
                wait(dve, yv_in[p], c.uses(32))
                wait(dve, fin_dve, c.n(FIN, -1))
                v.tensor_tensor(acc1[:], yv[:, p, 0], x12[:, bass.ds(c.n(RT), RT), :], ALU.add).then_inc(fin_dve, 1)
                wait(dve, fin_act, c.n(RT, -RT))
                wait(dve, fin_dve, c.n(FIN, 1))
                v.tensor_tensor(acc[:, p], acc1[:], yv[:, p, 1], ALU.add).then_inc(fin_dve, 1)
                wait(dve, fin_dve, c.n(FIN, 2))
                for t in range(RT):
                    v.bn_stats(st3[:, t], acc[:, p, t]).then_inc(fin_dve, 1)
                wait_apart(dve, fin_dve, c.n(FIN, 2 + RT), S["apart_dve"])
                for t in range(RT):
                    v.bn_aggr(mv3[:, p, t], st3[:, t]).then_inc(fin_dve, 1)

            in_fours(dve, NB // 2, step, before=0, after=0)


_INS = ['L0_attn_x', 'L0_attn_wq', 'L0_attn_wk_down', 'L0_attn_wv_down', 'L0_attn_wk_up', 'L0_attn_wv_up', 'L0_attn_wo',
        'L0_ffn_g1', 'L0_ffn_be1', 'L0_ffn_mix_w', 'L0_ffn_mix_b', 'L0_ffn_g2', 'L0_ffn_be2', 'L0_ffn_router_w',
        'L0_ffn_w1', 'L0_ffn_b1', 'L0_ffn_w2', 'L0_ffn_b2']


def kernel(**inputs):
    import numpy as np
    import concourse.bacc as bacc
    from concourse.bass_utils import run_bass_kernel_spmd

    nc = bacc.Bacc("TRN2", target_bir_lowering=False, num_devices=1)
    arrays, args = {}, []
    for name in _INS:
        a = np.ascontiguousarray(inputs[name])
        arrays[f"in_{name}"] = a
        args.append(nc.dram_tensor(f"in_{name}", a.shape, mybir.dt.from_np(a.dtype), kind="ExternalInput").ap())
    shape = inputs["L0_attn_x"].shape
    args.append(nc.dram_tensor("out_0", shape, F32, kind="ExternalOutput").ap())
    build(nc, *args)
    r = run_bass_kernel_spmd(nc, [arrays], core_ids=[0])
    return r.results[0]["out_0"]
```
